# Optimizing a Trainium2 kernel written in Bass

```python
import numpy as np
import jax
import jax.numpy as jnp

def _softmax(x, axis=-1):
    return jax.nn.softmax(x, axis=axis)

def _gelu(x):
    return jax.nn.gelu(x, approximate=True)

def _silu(x):
    return jax.nn.silu(x)

def _sigmoid(x):
    return jax.nn.sigmoid(x)

def _layernorm(x, axis=-1, eps=1e-05):
    m = jnp.mean(x, axis=axis, keepdims=True)
    v = jnp.var(x, axis=axis, keepdims=True)
    return (x - m) / jnp.sqrt(v + eps)

def _scatter_add(tgt, idx, src, axis=0):
    return tgt.at[idx].add(src)

def _segment_sum(src, seg, n):
    return jax.ops.segment_sum(src, seg, n)
kernel_name = 'mk_decoder_postln_d1_seqx_r4_195c32'

def setup_inputs(seed: int=0):
    np.random.seed(seed)
    _w = jnp.asarray

    def _rec_inputs():
        import jax
        import jax.numpy as jnp
        _rk = jax.random.key(seed)
        x = 7.22e-05 + 1 * jax.random.normal(jax.random.fold_in(_rk, 1), (4, 512, 512), jnp.float32)
        _lenS = 512 - jax.random.randint(jax.random.fold_in(_rk, 7), (4,), 0, max(1, 512 // 4) + 1, jnp.int32)
        _lenS2 = 512 - jax.random.randint(jax.random.fold_in(_rk, 8), (4,), 0, max(1, 512 // 4) + 1, jnp.int32)
        _ctx_1024P = jax.random.normal(jax.random.fold_in(_rk, 11), (4, 16, 256), jnp.float32)
        _ctx_1024c = jax.random.dirichlet(jax.random.fold_in(_rk, 511), 0.3 * jnp.ones((16,), jnp.float32), (4, 512))
        _ctx_1024t = jnp.einsum('bsk,bkd->bsd', _ctx_1024c, _ctx_1024P)
        _ctx_1024t = _ctx_1024t * jax.lax.rsqrt(jnp.mean(jnp.square(_ctx_1024t)) + 1e-12) * 0.953939
        ctx_1024 = -0.000673644 + 1.00013 * (_ctx_1024t + 0.3 * jax.random.normal(jax.random.fold_in(_rk, 611), (4, 512, 256), jnp.float32))
        return (x, ctx_1024)
    x, ctx_1024 = _rec_inputs()

    def _L0_attn_setup():
        import jax, jax.numpy as jnp
        import numpy as np
        import math
        B, S, E, H = (2, 512, 512, 16)
        HD = E // H // 2
        DEPTH = 12
        LAMBDA_INIT = 0.8 - 0.6 * math.exp(-0.3 * DEPTH)
        EPS = 1e-05

        def _rope_interleaved(x, cos, sin):
            xe, xo = (x[..., 0::2], x[..., 1::2])
            c = cos[None, :, None, :]
            s = sin[None, :, None, :]
            oe = xe * c - xo * s
            oo = xe * s + xo * c
            return jnp.stack([oe, oo], axis=-1).reshape(x.shape)
        key = jax.random.key(seed)
        ks = jax.random.split(key, 10)
        sc = 0.02
        return {'x': jax.random.normal(ks[0], (B, S, E), jnp.float32), 'Wq': jax.random.normal(ks[1], (E, E), jnp.float32) * sc, 'Wk': jax.random.normal(ks[2], (E, E), jnp.float32) * sc, 'Wv': jax.random.normal(ks[3], (E, E), jnp.float32) * sc, 'Wo': jax.random.normal(ks[4], (E, E), jnp.float32) * sc, 'lambda_q1': jax.random.normal(ks[5], (HD,), jnp.float32) * 0.1, 'lambda_k1': jax.random.normal(ks[6], (HD,), jnp.float32) * 0.1, 'lambda_q2': jax.random.normal(ks[7], (HD,), jnp.float32) * 0.1, 'lambda_k2': jax.random.normal(ks[8], (HD,), jnp.float32) * 0.1, 'gamma': jnp.ones((2 * HD,), jnp.float32)}
    _L0_attn_all = _L0_attn_setup()
    _L0_attn_in = {k: v for k, v in _L0_attn_all.items() if k in ('Wq', 'Wk', 'Wv', 'Wo', 'lambda_q1', 'lambda_k1', 'lambda_q2', 'lambda_k2', 'gamma')}
    del _L0_attn_all

    def _L0_xattn_setup():
        import jax, jax.numpy as jnp
        import numpy as np
        B, S1, S2, DCA = (2, 512, 256, 16)
        QDIM, KDIM, H = (512, 256, 16)
        HD = QDIM // H
        SCALE = HD ** (-0.5)
        EPS = 1e-06
        DCA_WEIGHT = 1.0

        def _ln(t, w, b):
            m = jnp.mean(t, axis=-1, keepdims=True)
            v = jnp.var(t, axis=-1, keepdims=True)
            return (t - m) * jax.lax.rsqrt(v + EPS) * w + b

        def _attn(q, k, v):
            s = jnp.einsum('bhqd,bhkd->bhqk', q, k) * SCALE
            p = jax.nn.softmax(s, axis=-1)
            return jnp.einsum('bhqk,bhkd->bhqd', p, v)
        key = jax.random.key(seed)
        ks = jax.random.split(key, 8)
        w = lambda k, shape: jax.random.normal(k, shape, jnp.float32) * 0.02
        return {'x': jax.random.normal(ks[0], (B, S1, QDIM), jnp.float32), 'y': jax.random.normal(ks[1], (B, S2 + DCA, KDIM), jnp.float32), 'Wq': w(ks[2], (QDIM, QDIM)), 'bq': jnp.zeros((QDIM,), jnp.float32), 'Wk': w(ks[3], (KDIM, QDIM)), 'bk': jnp.zeros((QDIM,), jnp.float32), 'Wv': w(ks[4], (KDIM, QDIM)), 'bv': jnp.zeros((QDIM,), jnp.float32), 'Wkv_dca': w(ks[5], (KDIM, 2 * QDIM)), 'bkv_dca': jnp.zeros((2 * QDIM,), jnp.float32), 'qn_w': jnp.ones((HD,), jnp.float32), 'qn_b': jnp.zeros((HD,), jnp.float32), 'kn_w': jnp.ones((HD,), jnp.float32), 'kn_b': jnp.zeros((HD,), jnp.float32), 'kn_dca_w': jnp.ones((HD,), jnp.float32), 'kn_dca_b': jnp.zeros((HD,), jnp.float32), 'Wo': w(ks[6], (QDIM, QDIM)), 'bo': jnp.zeros((QDIM,), jnp.float32)}
    _L0_xattn_all = _L0_xattn_setup()
    _L0_xattn_in = {k: v for k, v in _L0_xattn_all.items() if k in ('Wq', 'bq', 'Wk', 'bk', 'Wv', 'bv', 'Wkv_dca', 'bkv_dca', 'qn_w', 'qn_b', 'kn_w', 'kn_b', 'kn_dca_w', 'kn_dca_b', 'Wo', 'bo')}
    del _L0_xattn_all

    def _L0_ffn_setup():
        import jax, jax.numpy as jnp
        import numpy as np
        DIM = 512
        HID = 1408
        ZERO_POINT = 128.0

        def _qlinear(x, wq, scale):
            W = (wq.astype(jnp.float32) - ZERO_POINT) * scale[:, None]
            return jnp.einsum('bsd,hd->bsh', x, W)
        key = jax.random.key(seed)
        ks = jax.random.split(key, 7)
        B, S = (4, 512)
        sg = jax.random.uniform(ks[1], (HID,)) * (0.02 / np.sqrt(DIM)) + 0.0001
        su = jax.random.uniform(ks[3], (HID,)) * (0.02 / np.sqrt(DIM)) + 0.0001
        sd = jax.random.uniform(ks[5], (DIM,)) * (0.02 / np.sqrt(HID)) + 0.0001
        return {'x': jax.random.normal(ks[0], (B, S, DIM), dtype=jnp.float32), 'wq_gate': jax.random.randint(ks[2], (HID, DIM), 0, 64, dtype=jnp.int32), 's_gate': sg, 'wq_up': jax.random.randint(ks[4], (HID, DIM), 0, 64, dtype=jnp.int32), 's_up': su, 'wq_down': jax.random.randint(ks[6], (DIM, HID), 0, 64, dtype=jnp.int32), 's_down': sd}
    _L0_ffn_all = _L0_ffn_setup()
    _L0_ffn_in = {k: v for k, v in _L0_ffn_all.items() if k in ('wq_gate', 's_gate', 'wq_up', 's_up', 'wq_down', 's_down')}
    del _L0_ffn_all
    return {'x': x, 'ctx_1024': ctx_1024, 'L0_attn_Wq': _L0_attn_in['Wq'], 'L0_attn_Wk': _L0_attn_in['Wk'], 'L0_attn_Wv': _L0_attn_in['Wv'], 'L0_attn_Wo': _L0_attn_in['Wo'], 'L0_attn_lambda_q1': _L0_attn_in['lambda_q1'], 'L0_attn_lambda_k1': _L0_attn_in['lambda_k1'], 'L0_attn_lambda_q2': _L0_attn_in['lambda_q2'], 'L0_attn_lambda_k2': _L0_attn_in['lambda_k2'], 'L0_attn_gamma': _L0_attn_in['gamma'], 'L0_xattn_Wq': _L0_xattn_in['Wq'], 'L0_xattn_bq': _L0_xattn_in['bq'], 'L0_xattn_Wk': _L0_xattn_in['Wk'], 'L0_xattn_bk': _L0_xattn_in['bk'], 'L0_xattn_Wv': _L0_xattn_in['Wv'], 'L0_xattn_bv': _L0_xattn_in['bv'], 'L0_xattn_Wkv_dca': _L0_xattn_in['Wkv_dca'], 'L0_xattn_bkv_dca': _L0_xattn_in['bkv_dca'], 'L0_xattn_qn_w': _L0_xattn_in['qn_w'], 'L0_xattn_qn_b': _L0_xattn_in['qn_b'], 'L0_xattn_kn_w': _L0_xattn_in['kn_w'], 'L0_xattn_kn_b': _L0_xattn_in['kn_b'], 'L0_xattn_kn_dca_w': _L0_xattn_in['kn_dca_w'], 'L0_xattn_kn_dca_b': _L0_xattn_in['kn_dca_b'], 'L0_xattn_Wo': _L0_xattn_in['Wo'], 'L0_xattn_bo': _L0_xattn_in['bo'], 'L0_ffn_wq_gate': _L0_ffn_in['wq_gate'], 'L0_ffn_s_gate': _L0_ffn_in['s_gate'], 'L0_ffn_wq_up': _L0_ffn_in['wq_up'], 'L0_ffn_s_up': _L0_ffn_in['s_up'], 'L0_ffn_wq_down': _L0_ffn_in['wq_down'], 'L0_ffn_s_down': _L0_ffn_in['s_down']}

def reference(x, ctx_1024, L0_attn_Wq, L0_attn_Wk, L0_attn_Wv, L0_attn_Wo, L0_attn_lambda_q1, L0_attn_lambda_k1, L0_attn_lambda_q2, L0_attn_lambda_k2, L0_attn_gamma, L0_xattn_Wq, L0_xattn_bq, L0_xattn_Wk, L0_xattn_bk, L0_xattn_Wv, L0_xattn_bv, L0_xattn_Wkv_dca, L0_xattn_bkv_dca, L0_xattn_qn_w, L0_xattn_qn_b, L0_xattn_kn_w, L0_xattn_kn_b, L0_xattn_kn_dca_w, L0_xattn_kn_dca_b, L0_xattn_Wo, L0_xattn_bo, L0_ffn_wq_gate, L0_ffn_s_gate, L0_ffn_wq_up, L0_ffn_s_up, L0_ffn_wq_down, L0_ffn_s_down):
    import jax
    import jax.numpy as jnp

    def _L0_attn_ref(x, Wq, Wk, Wv, Wo, lambda_q1, lambda_k1, lambda_q2, lambda_k2, gamma):
        import jax, jax.numpy as jnp
        import numpy as np
        import math
        B, S, E, H = (2, 512, 512, 16)
        HD = E // H // 2
        DEPTH = 12
        LAMBDA_INIT = 0.8 - 0.6 * math.exp(-0.3 * DEPTH)
        EPS = 1e-05

        def _rope_interleaved(x, cos, sin):
            xe, xo = (x[..., 0::2], x[..., 1::2])
            c = cos[None, :, None, :]
            s = sin[None, :, None, :]
            oe = xe * c - xo * s
            oo = xe * s + xo * c
            return jnp.stack([oe, oo], axis=-1).reshape(x.shape)
        b, t, _ = x.shape
        angle = 1.0 / 2500 ** jnp.linspace(0.0, 1.0, HD // 2, dtype=jnp.float32)
        freqs = jnp.arange(t, dtype=jnp.float32)[:, None] * angle
        cos, sin = (jnp.cos(freqs), jnp.sin(freqs))
        q = (x @ Wq.T).reshape(b, t, 2 * H, HD)
        k = (x @ Wk.T).reshape(b, t, 2 * H, HD)
        v = (x @ Wv.T).reshape(b, t, H, 2 * HD)
        q = _rope_interleaved(q, cos, sin)
        k = _rope_interleaved(k, cos, sin)
        q = q.reshape(b, t, H, 2, HD)
        k = k.reshape(b, t, H, 2, HD)
        q1, q2 = (q[:, :, :, 0], q[:, :, :, 1])
        k1, k2 = (k[:, :, :, 0], k[:, :, :, 1])
        scale = HD ** (-0.5)
        s1 = jnp.einsum('bthd,bshd->bhts', q1, k1) * scale
        p1 = jax.nn.softmax(s1, axis=-1)
        o1 = jnp.einsum('bhts,bshd->bthd', p1, v)
        s2 = jnp.einsum('bthd,bshd->bhts', q2, k2) * scale
        p2 = jax.nn.softmax(s2, axis=-1)
        o2 = jnp.einsum('bhts,bshd->bthd', p2, v)
        lam1 = jnp.exp(jnp.sum(lambda_q1 * lambda_k1))
        lam2 = jnp.exp(jnp.sum(lambda_q2 * lambda_k2))
        lam = lam1 - lam2 + LAMBDA_INIT
        attn = o1 - lam * o2
        rms = jax.lax.rsqrt(jnp.mean(attn * attn, axis=-1, keepdims=True) + EPS)
        attn = attn * rms * gamma
        attn = attn * (1.0 - LAMBDA_INIT)
        attn = attn.reshape(b, t, H * 2 * HD)
        return attn @ Wo.T

    def _L0_xattn_ref(x, y, Wq, bq, Wk, bk, Wv, bv, Wkv_dca, bkv_dca, qn_w, qn_b, kn_w, kn_b, kn_dca_w, kn_dca_b, Wo, bo):
        import jax, jax.numpy as jnp
        import numpy as np
        B, S1, S2, DCA = (2, 512, 256, 16)
        QDIM, KDIM, H = (512, 256, 16)
        HD = QDIM // H
        SCALE = HD ** (-0.5)
        EPS = 1e-06
        DCA_WEIGHT = 1.0

        def _ln(t, w, b):
            m = jnp.mean(t, axis=-1, keepdims=True)
            v = jnp.var(t, axis=-1, keepdims=True)
            return (t - m) * jax.lax.rsqrt(v + EPS) * w + b

        def _attn(q, k, v):
            s = jnp.einsum('bhqd,bhkd->bhqk', q, k) * SCALE
            p = jax.nn.softmax(s, axis=-1)
            return jnp.einsum('bhqk,bhkd->bhqd', p, v)
        b, s1, _ = x.shape
        y_dca = y[:, -DCA:, :]
        y_main = y[:, :-DCA, :]
        kv_dca = (y_dca @ Wkv_dca + bkv_dca).reshape(b, DCA, 2, H, HD)
        k_dca = _ln(kv_dca[:, :, 0], kn_dca_w, kn_dca_b)
        v_dca = kv_dca[:, :, 1]
        s2 = y_main.shape[1]
        q = _ln((x @ Wq + bq).reshape(b, s1, H, HD), qn_w, qn_b)
        kv = jnp.concatenate([y_main @ Wk + bk, y_main @ Wv + bv], axis=-1)
        kv = kv.reshape(b, s2, H, 2 * HD)
        k = _ln(kv[..., :HD], kn_w, kn_b)
        v = kv[..., HD:]
        qT = q.transpose(0, 2, 1, 3)
        ctx = _attn(qT, k.transpose(0, 2, 1, 3), v.transpose(0, 2, 1, 3))
        ctx = ctx.transpose(0, 2, 1, 3).reshape(b, s1, QDIM)
        ctx_dca = _attn(qT, k_dca.transpose(0, 2, 1, 3), v_dca.transpose(0, 2, 1, 3))
        ctx_dca = ctx_dca.transpose(0, 2, 1, 3).reshape(b, s1, QDIM)
        ctx = ctx + DCA_WEIGHT * ctx_dca
        return ctx @ Wo + bo

    def _L0_ffn_ref(x, wq_gate, s_gate, wq_up, s_up, wq_down, s_down):
        import jax, jax.numpy as jnp
        import numpy as np
        DIM = 512
        HID = 1408
        ZERO_POINT = 128.0

        def _qlinear(x, wq, scale):
            W = (wq.astype(jnp.float32) - ZERO_POINT) * scale[:, None]
            return jnp.einsum('bsd,hd->bsh', x, W)
        gate = _qlinear(x, wq_gate, s_gate)
        gate = jax.nn.silu(gate)
        up = _qlinear(x, wq_up, s_up)
        return _qlinear(gate * up, wq_down, s_down)
    x = _layernorm(x + _L0_attn_ref(x, L0_attn_Wq, L0_attn_Wk, L0_attn_Wv, L0_attn_Wo, L0_attn_lambda_q1, L0_attn_lambda_k1, L0_attn_lambda_q2, L0_attn_lambda_k2, L0_attn_gamma), axis=-1)
    x = _layernorm(x + _L0_xattn_ref(x, ctx_1024, L0_xattn_Wq, L0_xattn_bq, L0_xattn_Wk, L0_xattn_bk, L0_xattn_Wv, L0_xattn_bv, L0_xattn_Wkv_dca, L0_xattn_bkv_dca, L0_xattn_qn_w, L0_xattn_qn_b, L0_xattn_kn_w, L0_xattn_kn_b, L0_xattn_kn_dca_w, L0_xattn_kn_dca_b, L0_xattn_Wo, L0_xattn_bo), axis=-1)
    x = _layernorm(x + _L0_ffn_ref(x, L0_ffn_wq_gate, L0_ffn_s_gate, L0_ffn_wq_up, L0_ffn_s_up, L0_ffn_wq_down, L0_ffn_s_down), axis=-1)
    return x

_drawn_inputs = setup_inputs


def setup_inputs(seed=0):
    import zlib

    import numpy as np

    out = dict(_drawn_inputs(seed))
    spreads = {'L0_attn_gamma': (1.0, 0.6),
     'L0_xattn_bq': (0.0, 0.705),
     'L0_xattn_bk': (0.0, 0.1),
     'L0_xattn_bv': (0.0, 0.1),
     'L0_xattn_bkv_dca': (0.0, 0.1),
     'L0_xattn_qn_w': (1.0, 0.6),
     'L0_xattn_qn_b': (0.0, 0.8),
     'L0_xattn_kn_w': (1.0, 0.6),
     'L0_xattn_kn_b': (0.0, 2.0),
     'L0_xattn_kn_dca_w': (1.0, 0.6),
     'L0_xattn_kn_dca_b': (0.0, 2.0),
     'L0_xattn_bo': (0.0, 0.1)}
    factors = {'L0_attn_lambda_q1': 24.563,
     'L0_attn_lambda_q2': 200.0,
     'L0_attn_lambda_k2': 8.0,
     'L0_ffn_s_gate': 5.975,
     'L0_ffn_s_up': 6.724,
     'L0_ffn_s_down': 3.033}
    for name, (base, spread) in spreads.items():
        noise = np.random.default_rng([zlib.crc32(name.encode()), seed]).standard_normal(out[name].shape)
        drawn = base * np.exp(spread * noise) if base else spread * noise
        out[name] = jnp.asarray(drawn.astype(out[name].dtype))
    for name, factor in factors.items():
        out[name] = (out[name] * factor).astype(out[name].dtype)
    return out
```

```python
from contextlib import ExitStack

import concourse.bass as bass
from concourse import mybir

F32 = mybir.dt.float32
F32R = mybir.dt.float32r
I32 = mybir.dt.int32
ALU = mybir.AluOpType
ACT = mybir.ActivationFunctionType
AX_X = mybir.AxisListType.X
ENGINES = [mybir.EngineType.SP, mybir.EngineType.DVE, mybir.EngineType.Activation,
           mybir.EngineType.Pool, mybir.EngineType.PE]

P = 128
B, S, E = 4, 512, 512
H, HW = 16, 32
HD = HW // 2
PAIRS = HD // 2
CD, DCA = 256, 16
MAIN = S - DCA
HID = 1408
TT = S // P
EC = E // P
CC = CD // P
FC = HID // P
G = P // HW
ZERO_POINT = 128.0
LAMBDA_INIT = 0.8 - 0.6 * 2.718281828459045 ** (-0.3 * 12)
RMS_EPS, LN_EPS, HEAD_EPS = 1e-05, 1e-05, 1e-06
LOOP_SEMS = 180
DMA = 16


LN_AND_EXP = "natural_log_exp_and_others"


def loop_over_batch(nc, ctx, names, build):
    sems = {n: ctx.enter_context(nc.semaphore(n, num=LOOP_SEMS + i)) for i, n in enumerate(names)}
    with nc.Fori(0, B) as b:
        with nc.Block() as block:
            build(block, b, sems)
        nc.multi_engine_barrier(ENGINES, sems_to_clear=range(LOOP_SEMS, LOOP_SEMS + len(names)))


class Banks:

    def __init__(self, order, tiles, sems):
        self.at = {key: i for i, key in enumerate(order)}
        self.tiles, self.sems = tiles, sems

    @staticmethod
    def names(count):
        return [f"bank_full{n}" for n in range(count)]

    def tile(self, key):
        return self.tiles[self.at[key] % len(self.tiles)]

    def full(self, key):
        return self.sems[f"bank_full{self.at[key] % len(self.tiles)}"]

    def round(self, key):
        return self.at[key] // len(self.tiles)


def three_products(pe, out, weights, moving, first, last):
    (w_hi, w_lo), (m_hi, m_lo) = weights, moving
    pe.matmul(out, w_hi, m_hi, start=first, stop=False)
    pe.matmul(out, w_hi, m_lo, start=False, stop=False)
    return pe.matmul(out, w_lo, m_hi, start=False, stop=last)


def split_weights(nc, ctx, name, sources, width, integers=False, centre=()):
    hi = ctx.enter_context(nc.sbuf_tensor(f"{name}_hi", [P, width * len(sources)], F32R))
    lo = ctx.enter_context(nc.sbuf_tensor(f"{name}_lo", [P, width * len(sources)], F32R))
    where = {}
    slots = 4
    with ExitStack() as inner:
        raw = inner.enter_context(nc.sbuf_tensor(f"{name}_raw", [P, slots, width], I32 if integers else F32))
        mean = inner.enter_context(nc.sbuf_tensor(f"{name}_mean", [P, slots, width // HW], F32))
        raw_in = [inner.enter_context(nc.semaphore(f"{name}_raw_in{n}")) for n in range(slots)]
        hi_done = inner.enter_context(nc.semaphore(f"{name}_hi_done"))
        lo_done = inner.enter_context(nc.semaphore(f"{name}_lo_done"))
        centred = inner.enter_context(nc.semaphore(f"{name}_centred"))
        for n, (piece, _) in enumerate(sources):
            where[piece] = (hi[:, n * width:(n + 1) * width], lo[:, n * width:(n + 1) * width])
        with nc.Block() as block:
            @block.sync
            def _(sp):
                for n, (piece, src) in enumerate(sources):
                    if n >= slots:
                        sp.wait_ge(lo_done, n - slots + 1)
                    sp.dma_start(raw[:, n % slots, :], src).then_inc(raw_in[n % slots], DMA)

            @block.scalar
            def _(act):
                for n, (piece, _) in enumerate(sources):
                    if piece in centre:
                        act.wait_ge(centred, 2 * (1 + [p for p, _ in sources if p in centre].index(piece)))
                    act.wait_ge(raw_in[n % slots], DMA * (n // slots + 1))
                    if integers:
                        act.activation(where[piece][0], raw[:, n % slots, :], ACT.Copy,
                                       bias=-ZERO_POINT).then_inc(hi_done, 1)
                    else:
                        act.activation(where[piece][0], raw[:, n % slots, :], ACT.Copy).then_inc(hi_done, 1)

            @block.vector
            def _(dve):
                steps = 0
                for n, (piece, _) in enumerate(sources):
                    dve.wait_ge(raw_in[n % slots], DMA * (n // slots + 1))
                    full = raw[:, n % slots, :]
                    if piece in centre:
                        by_head = full.rearrange("p (h d) -> p h d", d=HW)
                        dve.tensor_reduce(mean[:, n % slots, :], by_head, AX_X, ALU.add).then_inc(centred, 1)
                        steps += 1
                        dve.wait_ge(centred, steps)
                        dve.scalar_tensor_tensor(
                            by_head, mean[:, n % slots, :].unsqueeze(2).broadcast_to([P, width // HW, HW]),
                            -1.0 / HW, by_head, ALU.mult, ALU.add).then_inc(centred, 1)
                        steps += 1
                        dve.wait_ge(centred, steps)
                    dve.wait_ge(hi_done, n + 1)
                    if integers:
                        dve.scalar_tensor_tensor(where[piece][1], full, -ZERO_POINT, where[piece][0].bitcast(F32),
                                                 ALU.add, ALU.subtract).then_inc(lo_done, 1)
                    else:
                        dve.tensor_tensor(where[piece][1], full, where[piece][0].bitcast(F32),
                                          ALU.subtract).then_inc(lo_done, 1)
    return where



def self_projections(nc, t, scratch):
    with ExitStack() as ctx:
        sources = [((m, k), t[m][k * P:(k + 1) * P, :]) for m in ("wq", "wk", "wv") for k in range(EC)]
        w = split_weights(nc, ctx, "w1", sources, E)
        sb = lambda n, shape, dt=F32: ctx.enter_context(nc.sbuf_tensor(n, shape, dt))
        trig = sb("trig", [P, 2, S])
        x_raw = sb("x_raw", [P, EC, S])
        x_hi, x_lo = sb("x_hi", [P, EC, S], F32R), sb("x_lo", [P, EC, S], F32R)
        products = sb("rope_products", [P, 2, 4, S])
        rotated = sb("rotated", [P, 2, 2 * S])
        parts = sb("parts", [P, 2, 2, 2 * S])
        v = sb("v_out", [P, TT, E])
        psum = [ctx.enter_context(nc.psum_tensor(f"ps1_{n}", [P, S], F32)) for n in range(8)]
        trig_in = ctx.enter_context(nc.semaphore("trig_in"))
        with nc.Block() as block:
            @block.sync
            def _(sp):
                sp.dma_start(trig[:, :, :], t["trig"]).then_inc(trig_in, DMA)
                sp.wait_ge(trig_in, DMA)

        turns = [("q", 0), ("k", 0), ("q", 1), ("k", 1)]
        order = [(*turns[0], 0), (*turns[0], 1), (*turns[1], 0), (*turns[1], 1)]
        order += [("v", n, 0) for n in range(TT)]
        order += [(*turns[2], 0), (*turns[2], 1), (*turns[3], 0), (*turns[3], 1)]
        names = [f"x_in{k}" for k in range(EC)] + ["x_hi_done", "x_lo_done", "products_ready", "rotated_ready",
                                                   "hi_done", "lo_done", "v_done", "parts_out0", "parts_out1",
                                                   "v_out_done"] + Banks.names(8)

        def build(block, b, sems):
            bank = Banks(order, psum, sems)

            @block.sync
            def _(sp):
                for k in range(EC):
                    sp.dma_start(x_raw[:, k, :], t["xT"][bass.ds(b, 1), k * P:(k + 1) * P, :]
                                 .rearrange("a p n -> p (a n)")).then_inc(sems[f"x_in{k}"], DMA)
                for n, (m, j) in enumerate(turns):
                    if n == 2:
                        sp.wait_ge(sems["v_done"], TT)
                        sp.dma_start(scratch["v"][bass.ds(b, 1)].rearrange("a p n -> p (a n)"),
                                     v[:, :, :].rearrange("p t n -> p (t n)")).then_inc(sems["v_out_done"], DMA)
                    sp.wait_ge(sems["lo_done"], n + 1)
                    sp.dma_start(scratch[m][bass.ds(b, 1), :, j].rearrange("a k (p e) n -> p (a k) e n", e=2),
                                 parts[:, n % 2].rearrange("p k (e n) -> p k e n", e=2)
                                 ).then_inc(sems[f"parts_out{n % 2}"], DMA)
                sp.wait_ge(sems["v_out_done"], DMA)
                sp.wait_ge(sems["parts_out0"], 2 * DMA)
                sp.wait_ge(sems["parts_out1"], 2 * DMA)

            @block.scalar
            def _(act):
                for k in range(EC):
                    act.wait_ge(sems[f"x_in{k}"], DMA)
                    act.activation(x_hi[:, k, :], x_raw[:, k, :], ACT.Copy).then_inc(sems["x_hi_done"], 1)

                def hi_part(n):
                    act.wait_ge(sems["rotated_ready"], n + 1)
                    if n >= 2:
                        act.wait_ge(sems[f"parts_out{n % 2}"], DMA * (n // 2))
                    act.activation(parts[:, n % 2, 0, :].bitcast(F32R), rotated[:, n % 2, :],
                                   ACT.Copy).then_inc(sems["hi_done"], 1)

                hi_part(0)
                hi_part(1)
                for n in range(TT):
                    act.wait_ge(bank.full(("v", n, 0)), bank.round(("v", n, 0)) + 1)
                    act.activation(v[:, n, :], bank.tile(("v", n, 0))[:, :], ACT.Copy).then_inc(sems["v_done"], 1)
                hi_part(2)
                hi_part(3)

            @block.gpsimd
            def _(pool):
                for n in range(len(turns)):
                    pool.wait_ge(sems["products_ready"], n + 1)
                    if n >= 2:
                        pool.wait_ge(sems["hi_done"], n - 1)
                    pool.tensor_tensor(rotated[:, n % 2, 0:S], products[:, n % 2, 0, :], products[:, n % 2, 1, :],
                                       ALU.subtract)
                    pool.tensor_tensor(rotated[:, n % 2, S:2 * S], products[:, n % 2, 2, :],
                                       products[:, n % 2, 3, :], ALU.add).then_inc(sems["rotated_ready"], 1)
                    pool.wait_ge(sems["hi_done"], n + 1)
                    pool.wait_ge(sems["rotated_ready"], n + 1)
                    pool.tensor_tensor(parts[:, n % 2, 1, :].bitcast(F32R), rotated[:, n % 2, :],
                                       parts[:, n % 2, 0, :], ALU.subtract).then_inc(sems["lo_done"], 1)

            @block.vector
            def _(dve):
                for k in range(EC):
                    dve.wait_ge(sems["x_hi_done"], k + 1)
                    dve.wait_ge(sems[f"x_in{k}"], DMA)
                    dve.tensor_tensor(x_lo[:, k, :], x_raw[:, k, :], x_hi[:, k, :].bitcast(F32),
                                      ALU.subtract).then_inc(sems["x_lo_done"], 1)
                for n, (m, j) in enumerate(turns):
                    even, odd = (m, j, 0), (m, j, 1)
                    if n >= 2:
                        dve.wait_ge(sems["rotated_ready"], n - 1)
                    dve.wait_ge(bank.full(even), bank.round(even) + 1)
                    dve.tensor_tensor(products[:, n % 2, 0, :], bank.tile(even)[:, :], trig[:, 0, :], ALU.mult)
                    dve.tensor_tensor(products[:, n % 2, 2, :], bank.tile(even)[:, :], trig[:, 1, :],
                                      ALU.mult)
                    dve.wait_ge(bank.full(odd), bank.round(odd) + 1)
                    dve.tensor_tensor(products[:, n % 2, 1, :], bank.tile(odd)[:, :], trig[:, 1, :],
                                      ALU.mult)
                    dve.tensor_tensor(products[:, n % 2, 3, :], bank.tile(odd)[:, :], trig[:, 0, :],
                                      ALU.mult).then_inc(sems["products_ready"], 1)

            @block.tensor
            def _(pe):
                for i, key in enumerate(order):
                    m, j, e = key
                    if bank.round(key):
                        pe.wait_ge(sems["products_ready"], i // 2 - 3)
                    for k in range(EC):
                        if i == 0:
                            pe.wait_ge(sems["x_hi_done"], k + 1)
                            pe.wait_ge(sems["x_lo_done"], k + 1)
                        xk = (x_hi[:, k, :], x_lo[:, k, :])
                        if m == "v":
                            xk = tuple(a[:, j * P:(j + 1) * P] for a in xk)
                            mm = three_products(pe, bank.tile(key)[:, :], xk, w["wv", k], k == 0, k == EC - 1)
                        else:
                            c = (2 * j + e) * P
                            wk = tuple(a[:, c:c + P] for a in w["w" + m, k])
                            mm = three_products(pe, bank.tile(key)[:, :], wk, xk, k == 0, k == EC - 1)
                    mm.then_inc(bank.full(key), 1)

        loop_over_batch(nc, ctx, names, build)



def attention(nc, t, scratch, kind):
    cross = kind == "cross"
    NH = H // G if cross else 2 * H // G
    RW = HW if cross else HD
    SCALE = float(RW) ** -0.5
    BIAS = 96
    ROWS = BIAS + (4 if cross else 2)
    NK = MAIN if cross else S
    NM = 2 * 16 if cross else 16
    STEPS = NH * TT
    SLOTS, PB = 3, 3
    with ExitStack() as ctx:
        sb = lambda n, shape, dt=F32: ctx.enter_context(nc.sbuf_tensor(f"{kind}_{n}", shape, dt))
        q_stack = sb("q_stack", [P, SLOTS, 4, S], F32R)
        k_stack = sb("k_stack", [P, SLOTS, 4, S], F32R)
        probs = sb("probs", [P, PB, 4, S])
        NV = TT + cross
        v = sb("v", [P, NV, E])
        ones = sb("ones", [P, HW])
        ident = sb("ident", [P, P])
        head_mean = sb("head_mean", [P, P])
        key_rows = sb("key_rows", [P, S])
        neg_max = sb("neg_max", [P, 2, NM])
        m_hi, m_lo = sb("m_hi", [P, 2, P]), sb("m_lo", [P, 2, P])
        log_sum = sb("log_sum", [P, S])
        inv_sum = sb("inv_sum", [P, S])
        first = sb("first", [P, S])
        out = sb("out", [P, 2, S])
        lam = sb("lam", [P, 4, HD])
        lam_sums = sb("lam_sums", [P, 2])
        lam_work = sb("lam_work", [P, 3, HD])
        neg_lam = sb("neg_lam", [P, 1])
        gamma = sb("gamma", [P, 2])
        diff = sb("diff", [P, 2, S])
        mean_sq = sb("mean_sq", [P, 2, S])
        ps_s = [ctx.enter_context(nc.psum_tensor(f"{kind}_ps_s{n}", [P, S], F32)) for n in range(2)]
        ps_t = [ctx.enter_context(nc.psum_tensor(f"{kind}_ps_t{n}", [P, 2 * S], F32)) for n in range(2)]
        ps_o = ctx.enter_context(nc.psum_tensor(f"{kind}_ps_o", [P, S], F32))
        ps_l = ctx.enter_context(nc.psum_tensor(f"{kind}_ps_l", [P, S], F32))

        sem = lambda n: ctx.enter_context(nc.semaphore(f"{kind}_{n}"))
        const_in, const_set, lam_in, lam_done = sem("const_in"), sem("const_set"), sem("lam_in"), sem("lam_done")
        with nc.Block() as block:
            @block.sync
            def _(sp):
                sp.dma_start(ident[:, :], t["ident"]).then_inc(const_in, DMA)
                sp.dma_start(head_mean[:, :], t["head_mean"]).then_inc(const_in, DMA)
                sp.dma_start(key_rows[BIAS:BIAS + 4, :], t["key_rows"]).then_inc(const_in, DMA)
                if not cross:
                    for n, name in enumerate(("lambda_q1", "lambda_k1", "lambda_q2", "lambda_k2")):
                        sp.dma_start(lam[:, n, :], t[name].partition_broadcast(P)).then_inc(lam_in, DMA)
                    sp.dma_start(gamma[:, 0:1], t["gamma"]).then_inc(lam_in, DMA)
                sp.wait_ge(const_in, 3 * DMA)

            @block.vector
            def _(dve):
                dve.memset(ones[:, :], 1.0)
                dve.memset(q_stack[:, :, :, :].bitcast(F32), 0.0)
                dve.memset(k_stack[:, :, :, :].bitcast(F32), 0.0).then_inc(const_set, 1)
                dve.wait_ge(const_set, 1)
                if cross:
                    dve.wait_ge(const_in, 3 * DMA)
                    for n in range(SLOTS):
                        for u in range(4):
                            dve.tensor_copy(k_stack[BIAS:ROWS, n, u, :], key_rows[BIAS:ROWS, :])
                else:
                    dve.memset(k_stack[BIAS:ROWS, :, :, :].bitcast(F32), 1.0)
                    dve.wait_ge(lam_in, 5 * DMA)
                    for n in range(2):
                        dve.tensor_tensor(lam_work[:, n, :], lam[:, 2 * n, :], lam[:, 2 * n + 1, :],
                                          ALU.mult).then_inc(lam_done, 1)
                    dve.wait_ge(lam_done, 2)
                    dve.tensor_reduce(lam_sums[:, :], lam_work[:, 0:2, :], AX_X, ALU.add).then_inc(lam_done, 1)
                    dve.tensor_scalar(gamma[:, 1:2], gamma[:, 0:1], 1.0 - LAMBDA_INIT, None, ALU.mult)
                    dve.wait_ge(lam_done, 4)
                    dve.scalar_tensor_tensor(neg_lam[:, :], lam_work[:, 2, 1:2], -LAMBDA_INIT, lam_work[:, 2, 0:1],
                                             ALU.add, ALU.subtract)

            @block.scalar
            def _(act):
                if not cross:
                    act.wait_ge(lam_done, 3)
                    act.activation(lam_work[:, 2, 0:2], lam_sums[:, :], ACT.Exp).then_inc(lam_done, 1)

        def early(h):
            return [("scores", h, u, n) for u in range(4) for n in range(TT)]

        uses = {-1: early(0) + [("maxima", 0)] + early(1) + [("maxima", 1)]}
        for h in range(NH):
            for c in range(TT):
                u = []
                if c == 0 and 2 <= h + 1 < NH:
                    u.append(("maxima", h + 1))
                if h + 2 < NH:
                    u += [("scores", h + 2, c, n) for n in range(TT)]
                if not cross and c == 2 and h % 2 == 0 and h:
                    u.append(("rms", h // 2 - 1))
                uses[TT * h + c] = u
        uses[STEPS] = [] if cross else [("rms", NH // 2 - 1)]
        use_at = {key: i for i, key in enumerate(k for st in range(-1, STEPS + 1) for k in uses[st])}

        products = {}
        for st in range(STEPS + 3):
            h, c = divmod(st, TT)
            if cross:
                products[st] = [[("pv", h - 1, 3)] if h else [], [("dca", h - 1)] if h else [],
                                [("pv", h, 0), ("pv", h, 1)], [("pv", h, 2)]][c]
                products[st] = [p for p in products[st] if p[1] < NH]
            else:
                products[st] = [("pv", *divmod(st - 1, TT))] if 1 <= st <= STEPS else []
        product_at = {key: i for i, key in enumerate(k for st in range(STEPS + 3) for k in products[st])}
        results = [k for k in product_at if k[0] == "dca" or k[2] == TT - 1]
        result_at = {key: i for i, key in enumerate(results)}

        names = ["v_in", "stack_in0", "stack_in1", "stack_in2", "bias_in0", "bias_in1", "bias_in2",
                 "scores_ready", "scores_read", "turned_hi", "shifted_ready",
                 "exp_done", "products_done", "log_done", "inverse_done", "output_read",
                 "diff_done", "squares_done", "rms_log", "rms_done", "out_done",
                 "out_stored0", "out_stored1"]
        NOUT = NH if cross else NH // 2
        NB = 4 if cross else 2

        def build(block, b, sems):
            stack_in = [sems[f"stack_in{n}"] for n in range(SLOTS)]
            bias_in = [sems[f"bias_in{n}"] for n in range(SLOTS)]
            out_stored = [sems[f"out_stored{n}"] for n in range(2)]

            @block.sync
            def _(sp):
                def gather(h):
                    if h >= SLOTS:
                        sp.wait_ge(sems["shifted_ready"], 2 * TT * (h - SLOTS + 1))
                    for m, stack, kinds in (("q", q_stack, (0, 0, 1)), ("k", k_stack, (0, 1, 0))):
                        for term, part in enumerate(kinds):
                            if cross:
                                src = scratch["c" + m][bass.ds(b, 1), part, h]
                            else:
                                r0 = (h % 4) * 4 * HD
                                src = scratch[m][bass.ds(b, 1), part, h // 4, r0:r0 + 4 * HD]
                            sp.dma_start(stack[term * RW:(term + 1) * RW, h % SLOTS, :, :].bitcast(F32),
                                         src.rearrange("a (c r) n -> r (a c) n", c=4)
                                         ).then_inc(stack_in[h % SLOTS], DMA)

                def bias(h):
                    sp.wait_ge(sems["scores_read"], use_at["maxima", h] + 1)
                    for n in range(NB):
                        part = (m_hi, m_lo)[n % 2]
                        sp.dma_start(
                            q_stack[BIAS + n:BIAS + n + 1, h % SLOTS, :, :].bitcast(F32)
                            .rearrange("a u (t n) -> a (u t) n", t=TT),
                            part[16 * (n // 2):16 * (n // 2) + 16, h % 2, :]).then_inc(bias_in[h % SLOTS], DMA)

                def store(g):
                    sp.wait_ge(sems["out_done"], g + 1)
                    sp.dma_start(scratch["ctx" if cross else "attn"][bass.ds(b, 1), g]
                                 .rearrange("a p n -> p (a n)"), out[:, g % 2, :]).then_inc(out_stored[g % 2], DMA)

                gather(0)
                gather(1)
                sp.dma_start(v[:, :, :].rearrange("p t n -> p (t n)"),
                             scratch["cv" if cross else "v"][bass.ds(b, 1)].rearrange("a p n -> p (a n)")
                             ).then_inc(sems["v_in"], DMA)
                gather(2)
                bias(0)
                bias(1)
                for h in range(NH):
                    if h + 2 < NH:
                        if h + 3 < NH:
                            gather(h + 3)
                        bias(h + 2)
                    if not cross and h % 2 == 0 and h:
                        store(h // 2 - 1)
                    if cross and h:
                        store(h - 1)
                store(NOUT - 1)
                for n in range(2):
                    sp.wait_ge(out_stored[n], DMA * ((NOUT + 1 - n) // 2))

            @block.tensor
            def _(pe):
                def run(key):
                    i = use_at[key]
                    if i >= 2:
                        pe.wait_ge(sems["scores_read"], i - 1)
                    bank = ps_s[i % 2]
                    if key[0] == "scores":
                        _, h, u, n = key
                        if u == 0 and n == 0:
                            pe.wait_ge(stack_in[h % SLOTS], 6 * DMA * (h // SLOTS + 1))
                        pe.matmul(bank[:, :], q_stack[0:BIAS, h % SLOTS, u, n * P:(n + 1) * P],
                                  k_stack[0:BIAS, h % SLOTS, u, :], start=True, stop=True
                                  ).then_inc(sems["scores_ready"], 1)
                    elif key[0] == "maxima":
                        pe.wait_ge(sems["scores_read"], use_at["scores", key[1], 3, TT - 1] + 1)
                        pe.transpose(bank[0:NM, 0:P], neg_max[:, key[1] % 2, :], ident[:, :]
                                     ).then_inc(sems["scores_ready"], 1)
                    else:
                        pe.wait_ge(sems["squares_done"], key[1] + 1)
                        pe.matmul(bank[:, :], head_mean[:, :], mean_sq[:, 0, :], start=True, stop=True
                                  ).then_inc(sems["scores_ready"], 1)

                def shifted(h, c):
                    if c == 0:
                        pe.wait_ge(bias_in[h % SLOTS], NB * DMA * (h // SLOTS + 1))
                    for pair in range(2):
                        e = 2 * (TT * h + c) + pair
                        if e >= 2:
                            pe.wait_ge(sems["exp_done"], e - 1)
                        for i in range(2):
                            mm = pe.matmul(ps_t[pair][:, i * S:(i + 1) * S],
                                           k_stack[0:ROWS, h % SLOTS, 2 * pair + i, c * P:(c + 1) * P],
                                           q_stack[0:ROWS, h % SLOTS, 2 * pair + i, :], start=True, stop=True)
                        mm.then_inc(sems["shifted_ready"], 1)

                def product(key):
                    h = key[1]
                    c = TT - 1 if key[0] == "dca" else key[2]
                    st = TT * h + c
                    pe.wait_ge(sems["exp_done"], 2 * (st + 1))
                    if key == ("pv", 0, 0):
                        pe.wait_ge(sems["v_in"], DMA)
                    begins = key[0] == "dca" or c == 0
                    ends = key[0] == "dca" or c == TT - 1
                    if begins:
                        n = len([k for k in results if product_at[k] < product_at[key]])
                        if n:
                            pe.wait_ge(sems["output_read"], n)
                            pe.wait_ge(sems["log_done"], n)
                    tile = TT if key[0] == "dca" else c
                    for u in range(4):
                        head = 4 * h + u if cross else G * (h // 2) + u
                        pe.matmul(ps_o[HW * u:HW * (u + 1), :], v[:, tile, head * HW:(head + 1) * HW],
                                  probs[:, st % PB, u, :], start=begins, stop=ends)
                    for u in range(4):
                        w = key_ones(key, c)
                        mm = pe.matmul(ps_l[HW * u:HW * (u + 1), :], w, probs[:, st % PB, u, :],
                                       start=begins, stop=ends)
                    mm.then_inc(sems["products_done"], 1)

                def key_ones(key, c):
                    if not cross or c < TT - 1:
                        return ones[:, :]
                    return last_keys[:, 1 if key[0] == "dca" else 0, :]

                for key in uses[-1]:
                    run(key)
                for st in range(STEPS + 3):
                    if st < STEPS:
                        shifted(*divmod(st, TT))
                    for key in uses.get(st, []) if st < STEPS else []:
                        run(key)
                    for key in products[st]:
                        product(key)
                for key in uses[STEPS]:
                    run(key)

            @block.scalar
            def _(act):
                def inverse(key):
                    n = result_at[key]
                    act.wait_ge(sems["products_done"], product_at[key] + 1)
                    act.activation(log_sum[:, :], ps_l[:, :], ACT.Ln).then_inc(sems["log_done"], 1)
                    act.wait_ge(sems["log_done"], n + 1)
                    if n:
                        act.wait_ge(sems["output_read"], n)
                    act.activation(inv_sum[:, :], log_sum[:, :], ACT.Exp, scale=-1.0).then_inc(sems["inverse_done"], 1)

                def rms(g):
                    act.wait_ge(sems["scores_read"], use_at["rms", g] + 1)
                    act.activation(mean_sq[:, 0, :], mean_sq[:, 1, :], ACT.Ln).then_inc(sems["rms_log"], 1)
                    act.wait_ge(sems["rms_log"], g + 1)
                    act.activation(mean_sq[:, 1, :], mean_sq[:, 0, :], ACT.Exp, scale=-0.5).then_inc(sems["rms_done"], 1)

                nc.scalar.preload_act_table_set(LN_AND_EXP)
                for st in range(STEPS + 3):
                    if st < STEPS:
                        for pair in range(2):
                            act.wait_ge(sems["shifted_ready"], 2 * st + pair + 1)
                            if st >= PB and pair == 0:
                                h, c = divmod(st - PB, TT)
                                last = ("dca", h) if cross and c == TT - 1 else ("pv", h, c)
                                act.wait_ge(sems["products_done"], product_at[last] + 1)
                            act.activation(probs[:, st % PB, 2 * pair:2 * pair + 2, :].rearrange("p u n -> p (u n)"),
                                           ps_t[pair][:, :], ACT.Exp, scale=SCALE).then_inc(sems["exp_done"], 1)
                    for key in products[st]:
                        if key in result_at:
                            inverse(key)
                    if not cross and st % (2 * TT) == 3 and st > 3 and st < STEPS:
                        rms(st // (2 * TT) - 1)
                if not cross:
                    rms(NH // 2 - 1)

            @block.vector
            def _(dve):
                def read(key):
                    i = use_at[key]
                    bank = ps_s[i % 2]
                    dve.wait_ge(sems["scores_ready"], i + 1)
                    if key[0] == "scores":
                        _, h, u, n = key
                        if u == 0 and n == 0 and h >= 2:
                            dve.wait_ge(sems["scores_ready"], use_at["maxima", h - 2] + 1)
                        col = 4 * u + n
                        if cross:
                            dve.tensor_reduce(neg_max[:, h % 2, col:col + 1], bank[:, 0:NK], AX_X, ALU.max,
                                              negate=True)
                            red = dve.tensor_reduce(neg_max[:, h % 2, 16 + col:17 + col], bank[:, NK:S], AX_X,
                                                    ALU.max, negate=True)
                        else:
                            red = dve.tensor_reduce(neg_max[:, h % 2, col:col + 1], bank[:, :], AX_X, ALU.max,
                                                    negate=True)
                        red.then_inc(sems["scores_read"], 1)
                    elif key[0] == "maxima":
                        h = key[1]
                        if h >= 2:
                            dve.wait_ge(bias_in[(h - 2) % SLOTS], NB * DMA * ((h - 2) // SLOTS + 1))
                        dve.tensor_copy(m_hi[0:NM, h % 2, :].bitcast(F32R), bank[0:NM, 0:P]
                                        ).then_inc(sems["turned_hi"], 1)
                        dve.wait_ge(sems["turned_hi"], h + 1)
                        dve.tensor_tensor(m_lo[0:NM, h % 2, :].bitcast(F32R), bank[0:NM, 0:P],
                                          m_hi[0:NM, h % 2, :], ALU.subtract).then_inc(sems["scores_read"], 1)
                    else:
                        g = key[1]
                        if g:
                            dve.wait_ge(sems["out_done"], g)
                        dve.tensor_scalar(mean_sq[:, 1, :], bank[:, :], RMS_EPS, None, ALU.add
                                          ).then_inc(sems["scores_read"], 1)

                def normalise(key):
                    n = result_at[key]
                    dve.wait_ge(sems["inverse_done"], n + 1)
                    dve.wait_ge(sems["products_done"], product_at[key] + 1)
                    if n % 2 == 0:
                        if n:
                            dve.wait_ge(sems["out_done"] if cross else sems["diff_done"], n // 2)
                        dve.tensor_tensor(first[:, :], ps_o[:, :], inv_sum[:, :], ALU.mult
                                          ).then_inc(sems["output_read"], 1)
                        return
                    g = n // 2
                    dve.tensor_tensor(diff[:, 0, :], ps_o[:, :], inv_sum[:, :], ALU.mult).then_inc(sems["output_read"], 1)
                    dve.wait_ge(sems["output_read"], n + 1)
                    if cross:
                        if g >= 2:
                            dve.wait_ge(out_stored[g % 2], DMA * (g // 2))
                        dve.tensor_tensor(out[:, g % 2, :], diff[:, 0, :], first[:, :], ALU.add
                                          ).then_inc(sems["out_done"], 1)
                        return
                    dve.scalar_tensor_tensor(diff[:, 1, :], diff[:, 0, :], neg_lam[:, 0:1], first[:, :],
                                             ALU.mult, ALU.add).then_inc(sems["diff_done"], 1)
                    dve.wait_ge(sems["diff_done"], g + 1)
                    if g:
                        dve.wait_ge(sems["rms_done"], g)
                    dve.tensor_tensor(mean_sq[:, 0, :], diff[:, 1, :], diff[:, 1, :], ALU.mult
                                      ).then_inc(sems["squares_done"], 1)

                def finish(g):
                    dve.wait_ge(sems["rms_done"], g + 1)
                    if g >= 2:
                        dve.wait_ge(out_stored[g % 2], DMA * (g // 2))
                    dve.scalar_tensor_tensor(out[:, g % 2, :], diff[:, 1, :], gamma[:, 1:2], mean_sq[:, 1, :],
                                             ALU.mult, ALU.mult).then_inc(sems["out_done"], 1)

                for key in uses[-1]:
                    read(key)
                for st in range(STEPS + 3):
                    for key in products.get(st - 1, []):
                        if key in result_at:
                            normalise(key)
                    for key in uses.get(st, []) if st < STEPS else []:
                        read(key)
                    if not cross and st % (2 * TT) == 3 and 3 < st < STEPS:
                        finish(st // (2 * TT) - 1)
                for key in uses[STEPS]:
                    read(key)
                if not cross:
                    finish(NH // 2 - 1)

        if cross:
            last_keys = sb("last_keys", [P, 2, HW])
            masks = sb("masks", [P, 2])
            mask_in, mask_set = sem("mask_in"), sem("mask_set")
            with nc.Block() as block:
                @block.sync
                def _(sp):
                    sp.dma_start(masks[:, :], t["masks"]).then_inc(mask_in, DMA)

                @block.vector
                def _(dve):
                    dve.wait_ge(mask_in, DMA)
                    for n in range(2):
                        dve.tensor_scalar(last_keys[:, n, :], ones[:, :], masks[:, n:n + 1], None, ALU.mult)
        loop_over_batch(nc, ctx, names, build)



def middle(nc, t, scratch):
    with ExitStack() as ctx:
        sources = [(("wo", k), t["wo"][k * P:(k + 1) * P, :]) for k in range(EC)]
        sources += [(("xwq", k), t["xwq"][k * P:(k + 1) * P, :]) for k in range(EC)]
        for m in ("xwk", "xwv"):
            sources += [((m, k), t[m][k * P:(k + 1) * P, :]) for k in range(CC)]
        for m, c in (("xwk_dca", 0), ("xwv_dca", E)):
            sources += [((m, k), t["xwkv_dca"][k * P:(k + 1) * P, c:c + E]) for k in range(CC)]
        centre = [p for p, _ in sources if p[0] in ("xwq", "xwk", "xwk_dca")]
        w = split_weights(nc, ctx, "w3", sources, E, centre=centre)

        sb = lambda n, shape, dt=F32: ctx.enter_context(nc.sbuf_tensor(f"m_{n}", shape, dt))
        DEPTH = 4
        a_raw = sb("a_raw", [P, EC, S])
        y_hi, y_lo = sb("y_hi", [P, EC, S], F32R), sb("y_lo", [P, EC, S], F32R)
        c_raw = sb("c_raw", [P, CC, S])
        c_hi, c_lo = sb("c_hi", [P, CC, S], F32R), sb("c_lo", [P, CC, S], F32R)
        x_in = sb("x_in", [P, TT, E])
        centred = sb("centred", [P, DEPTH, S])
        squares = sb("squares", [P, DEPTH, S])
        scale = sb("scale", [P, DEPTH, S])
        normed = sb("normed", [P, 2, S])
        parts = sb("parts", [P, 2, 2, S])
        v = sb("v", [P, 2, E])
        bv = sb("bv", [P, 2, E])
        stats = sb("stats", [P, TT, 6])
        moments = sb("moments", [P, TT, 2])
        log_var = sb("log_var", [P, TT])
        rstd = sb("rstd", [P, TT])
        ident, head_mean, centring = sb("ident", [P, P]), sb("head_mean", [P, P]), sb("centring", [P, P])
        bias_raw, bias = sb("bias_raw", [P, 3, EC]), sb("bias", [P, 3, EC])
        affine = sb("affine", [P, 6])
        masks = sb("masks", [P, 2])
        eps = sb("eps", [P, 2])
        psum = [ctx.enter_context(nc.psum_tensor(f"ps3_{n}", [P, S], F32)) for n in range(8)]

        const_in = ctx.enter_context(nc.semaphore("m_const_in"))
        bias_ready = ctx.enter_context(nc.semaphore("m_bias_ready"))
        with nc.Block() as block:
            @block.sync
            def _(sp):
                for tile, name in ((ident, "ident"), (head_mean, "head_mean"), (centring, "centring"),
                                   (masks, "masks")):
                    sp.dma_start(tile[:, :], t[name]).then_inc(const_in, DMA)
                sp.dma_start(bias_raw[:, :, :], t["head_bias"]).then_inc(const_in, DMA)
                sp.dma_start(affine[:, :], t["head_affine"]).then_inc(const_in, DMA)
                sp.dma_start(bv[:, 0, :], t["xbv"].partition_broadcast(P)).then_inc(const_in, DMA)
                sp.dma_start(bv[:, 1, :], t["xbkv_dca"][E:2 * E].partition_broadcast(P)).then_inc(const_in, DMA)
                sp.wait_ge(const_in, 8 * DMA)

            @block.vector
            def _(dve):
                dve.memset(eps[:, 0:1], LN_EPS)
                dve.memset(eps[:, 1:2], HEAD_EPS)
                dve.wait_ge(bias_ready, 1)
                dve.tensor_copy(bias[:, :, :].rearrange("p n k -> p (n k)"), psum[0][:, 0:3 * EC])

            @block.tensor
            def _(pe):
                pe.wait_ge(const_in, 8 * DMA)
                pe.matmul(psum[0][:, 0:3 * EC], centring[:, :], bias_raw[:, :, :].rearrange("p n k -> p (n k)"),
                          start=True, stop=True).then_inc(bias_ready, 1)

        heads = [("k", j) for j in range(EC)] + [("q", j) for j in range(EC)]
        order = [("wo", n) for n in range(TT)] + [("k", j) for j in range(EC)] + [("v", n) for n in range(TT + 1)]
        order += [("turn", k) for k in range(EC)] + [("kvar", j) for j in range(EC)]
        order += [("q", 0), ("q", 1), ("qvar", 0), ("q", 2), ("qvar", 1), ("q", 3), ("qvar", 2), ("qvar", 3)]
        names = ["a_in", "c_in", "x_in", "a_hi", "a_lo", "c_hi", "c_lo", "z_done", "stats_done", "moments_done",
                 "log_done", "rstd_done", "x1_done", "x1_out", "y_hi_done", "y_lo_done", "centred_done",
                 "squares_done", "head_log", "scale_done", "scaled_done", "normed_done", "hi_done", "lo_done",
                 "parts_out0", "parts_out1", "v_done", "vm_done", "v_out0", "v_out1"] + Banks.names(8)

        def build(block, b, sems):
            bank = Banks(order, psum, sems)
            parts_out = [sems["parts_out0"], sems["parts_out1"]]
            v_out = [sems["v_out0"], sems["v_out1"]]

            def full(eng, key):
                eng.wait_ge(bank.full(key), bank.round(key) + 1)

            @block.sync
            def _(sp):
                sp.dma_start(a_raw[:, :, :], scratch["attn"][bass.ds(b, 1)].rearrange("a k p n -> p (a k) n")
                             ).then_inc(sems["a_in"], DMA)
                sp.dma_start(x_in[:, :, :], t["x"][bass.ds(b, 1)].rearrange("a (t p) e -> p (a t) e", p=P)
                             ).then_inc(sems["x_in"], DMA)
                sp.dma_start(c_raw[:, :, :], t["cT"][bass.ds(b, 1)].rearrange("a (k p) n -> p (a k) n", p=P)
                             ).then_inc(sems["c_in"], DMA)
                for n in range(TT + 1):
                    sp.wait_ge(sems["v_done"], n + 1)
                    sp.dma_start(scratch["cv"][bass.ds(b, 1), :, n * E:(n + 1) * E].rearrange("a p n -> p (a n)"),
                                 v[:, n % 2, :]).then_inc(v_out[n % 2], DMA)
                for n, (m, j) in enumerate(heads):
                    if n == EC:
                        sp.wait_ge(sems["x1_done"], TT)
                        sp.dma_start(scratch["x1"][bass.ds(b, 1)].rearrange("a (t p) e -> p (a t) e", p=P),
                                     x_in[:, :, :]).then_inc(sems["x1_out"], DMA)
                    sp.wait_ge(sems["lo_done"], n + 1)
                    sp.dma_start(scratch["c" + m][bass.ds(b, 1), :, j].rearrange("a k p n -> p (a k) n"),
                                 parts[:, n % 2, :, :]).then_inc(parts_out[n % 2], DMA)
                sp.wait_ge(sems["x1_out"], DMA)
                for n in range(2):
                    sp.wait_ge(parts_out[n], len(heads) // 2 * DMA)
                    sp.wait_ge(v_out[n], (3 - n) * DMA)

            @block.scalar
            def _(act):
                nc.scalar.preload_act_table_set(LN_AND_EXP)
                act.wait_ge(sems["a_in"], DMA)
                for k in range(EC):
                    act.activation(y_hi[:, k, :], a_raw[:, k, :], ACT.Copy).then_inc(sems["a_hi"], 1)
                act.wait_ge(sems["c_in"], DMA)
                for k in range(CC):
                    act.activation(c_hi[:, k, :], c_raw[:, k, :], ACT.Copy).then_inc(sems["c_hi"], 1)

                def centre(n):
                    m, j = heads[n]
                    full(act, (m, j))
                    if n >= DEPTH:
                        act.wait_ge(sems["normed_done"], n - DEPTH + 1)
                    ps = bank.tile((m, j))
                    if m == "k":
                        act.activation(centred[:, n % DEPTH, 0:MAIN], ps[:, 0:MAIN], ACT.Identity,
                                       bias=bias[:, 1, j:j + 1])
                        act.activation(centred[:, n % DEPTH, MAIN:S], ps[:, MAIN:S], ACT.Identity,
                                       bias=bias[:, 2, j:j + 1]).then_inc(sems["centred_done"], 1)
                    else:
                        act.activation(centred[:, n % DEPTH, :], ps[:, :], ACT.Identity,
                                       bias=bias[:, 0, j:j + 1]).then_inc(sems["centred_done"], 1)
                    act.wait_ge(sems["centred_done"], n + 1)
                    if n >= DEPTH:
                        prev = heads[n - DEPTH]
                        full(act, (prev[0] + "var", prev[1]))
                    act.activation(squares[:, n % DEPTH, :], centred[:, n % DEPTH, :], ACT.Square
                                   ).then_inc(sems["squares_done"], 1)

                def inverse(n):
                    m, j = heads[n]
                    full(act, (m + "var", j))
                    if n >= DEPTH:
                        act.wait_ge(sems["scaled_done"], n - DEPTH + 1)
                    ps = bank.tile((m + "var", j))
                    act.activation(scale[:, n % DEPTH, :], ps[:, :], ACT.Ln, bias=eps[:, 1:2]
                                   ).then_inc(sems["head_log"], 1)
                    act.wait_ge(sems["head_log"], n + 1)
                    act.activation(scale[:, n % DEPTH, :], scale[:, n % DEPTH, :], ACT.Exp, scale=-0.5
                                   ).then_inc(sems["scale_done"], 1)

                def hi_part(n):
                    act.wait_ge(sems["normed_done"], n + 1)
                    if n >= 2:
                        act.wait_ge(parts_out[n % 2], n // 2 * DMA)
                    act.activation(parts[:, n % 2, 0, :].bitcast(F32R), normed[:, n % 2, :], ACT.Copy
                                   ).then_inc(sems["hi_done"], 1)

                for n in range(EC):
                    centre(n)
                act.wait_ge(sems["moments_done"], TT)
                act.activation(log_var[:, :], moments[:, :, 1], ACT.Ln, bias=eps[:, 0:1]).then_inc(sems["log_done"], 1)
                act.wait_ge(sems["log_done"], 1)
                act.activation(rstd[:, :], log_var[:, :], ACT.Exp, scale=-0.5).then_inc(sems["rstd_done"], 1)
                for k in range(EC):
                    full(act, ("turn", k))
                    act.activation(y_hi[:, k, :], bank.tile(("turn", k))[:, :], ACT.Copy).then_inc(sems["y_hi_done"], 1)
                inverse(0)
                inverse(1)
                hi_part(0)
                inverse(2)
                hi_part(1)
                inverse(3)
                hi_part(2)
                hi_part(3)
                centre(4)
                centre(5)
                inverse(4)
                hi_part(4)
                centre(6)
                inverse(5)
                hi_part(5)
                centre(7)
                inverse(6)
                hi_part(6)
                inverse(7)
                hi_part(7)

            @block.gpsimd
            def _(pool):
                for n in range(len(heads)):
                    pool.wait_ge(sems["normed_done"], n + 1)
                    pool.wait_ge(sems["hi_done"], n + 1)
                    pool.tensor_tensor(parts[:, n % 2, 1, :].bitcast(F32R), normed[:, n % 2, :],
                                       parts[:, n % 2, 0, :], ALU.subtract).then_inc(sems["lo_done"], 1)

            @block.vector
            def _(dve):
                dve.wait_ge(sems["a_in"], DMA)
                for k in range(EC):
                    dve.wait_ge(sems["a_hi"], k + 1)
                    dve.tensor_tensor(y_lo[:, k, :], a_raw[:, k, :], y_hi[:, k, :].bitcast(F32), ALU.subtract
                                      ).then_inc(sems["a_lo"], 1)
                dve.wait_ge(sems["c_in"], DMA)
                for k in range(CC):
                    dve.wait_ge(sems["c_hi"], k + 1)
                    dve.tensor_tensor(c_lo[:, k, :], c_raw[:, k, :], c_hi[:, k, :].bitcast(F32), ALU.subtract
                                      ).then_inc(sems["c_lo"], 1)
                z = a_raw
                dve.wait_ge(sems["a_lo"], EC)
                dve.wait_ge(sems["x_in"], DMA)
                for n in range(TT):
                    full(dve, ("wo", n))
                    dve.tensor_tensor(z[:, n, :], bank.tile(("wo", n))[:, :], x_in[:, n, :], ALU.add
                                      ).then_inc(sems["z_done"], 1)
                    dve.wait_ge(sems["z_done"], n + 1)
                    dve.bn_stats(stats[:, n, :], z[:, n, :]).then_inc(sems["stats_done"], 1)
                    dve.wait_ge(sems["stats_done"], n + 1)
                    dve.bn_aggr(moments[:, n, :], stats[:, n, :]).then_inc(sems["moments_done"], 1)
                dve.wait_ge(sems["moments_done"], TT)
                dve.wait_ge(sems["rstd_done"], 1)
                for n in range(TT):
                    dve.tensor_scalar(x_in[:, n, :], z[:, n, :], moments[:, n, 0:1], rstd[:, n:n + 1],
                                      ALU.subtract, ALU.mult).then_inc(sems["x1_done"], 1)

                def affine_norm(n):
                    m, j = heads[n]
                    dve.wait_ge(sems["centred_done"], n + 1)
                    dve.wait_ge(sems["scale_done"], n + 1)
                    dve.tensor_tensor(centred[:, n % DEPTH, :], centred[:, n % DEPTH, :], scale[:, n % DEPTH, :], ALU.mult
                                      ).then_inc(sems["scaled_done"], 1)
                    dve.wait_ge(sems["scaled_done"], n + 1)
                    if n >= 2:
                        dve.wait_ge(sems["lo_done"], n - 1)
                    if m == "k":
                        dve.tensor_scalar(normed[:, n % 2, 0:MAIN], centred[:, n % DEPTH, 0:MAIN],
                                          affine[:, 2:3], affine[:, 3:4], ALU.mult, ALU.add)
                        dve.tensor_scalar(normed[:, n % 2, MAIN:S], centred[:, n % DEPTH, MAIN:S],
                                          affine[:, 4:5], affine[:, 5:6], ALU.mult, ALU.add
                                          ).then_inc(sems["normed_done"], 1)
                    else:
                        dve.tensor_scalar(normed[:, n % 2, :], centred[:, n % DEPTH, :],
                                          affine[:, 0:1], affine[:, 1:2], ALU.mult, ALU.add
                                          ).then_inc(sems["normed_done"], 1)

                for n in range(TT + 1):
                    key = ("v", n)
                    full(dve, key)
                    if n >= 2:
                        dve.wait_ge(v_out[n % 2], n // 2 * DMA)
                    done = sems["v_done"] if n < TT - 1 else sems["vm_done"]
                    dve.tensor_tensor(v[:, n % 2, :], bank.tile(key)[:, :], bv[:, n // TT, :], ALU.add
                                      ).then_inc(done, 1)
                    if n >= TT - 1:
                        dve.wait_ge(sems["vm_done"], n - TT + 2)
                        dve.tensor_scalar(v[:, n % 2, :], v[:, n % 2, :], masks[:, n // TT:n // TT + 1], None,
                                          ALU.mult).then_inc(sems["v_done"], 1)
                for k in range(EC):
                    full(dve, ("turn", k))
                    dve.wait_ge(sems["y_hi_done"], k + 1)
                    dve.tensor_tensor(y_lo[:, k, :], bank.tile(("turn", k))[:, :], y_hi[:, k, :].bitcast(F32),
                                      ALU.subtract).then_inc(sems["y_lo_done"], 1)
                for n in range(len(heads)):
                    affine_norm(n)

            @block.tensor
            def _(pe):
                for key in order:
                    m, j = key
                    ps = bank.tile(key)
                    if bank.round(key):
                        prev = order[bank.at[key] - 8]
                        if prev[0] in ("k", "q"):
                            pe.wait_ge(sems["centred_done"], heads.index(prev) + 1)
                        elif prev[0] == "v":
                            pe.wait_ge(sems["v_done"], min(prev[1] + 1, TT - 1))
                            if prev[1] >= TT - 1:
                                pe.wait_ge(sems["vm_done"], prev[1] - TT + 2)
                        elif prev[0] == "turn":
                            pe.wait_ge(sems["y_lo_done"], prev[1] + 1)
                        elif prev[0] == "wo":
                            pe.wait_ge(sems["z_done"], prev[1] + 1)
                        else:
                            pe.wait_ge(sems["head_log"], heads.index((prev[0][0], prev[1])) + 1)
                    if m == "wo":
                        for k in range(EC):
                            pe.wait_ge(sems["a_hi"], k + 1)
                            pe.wait_ge(sems["a_lo"], k + 1)
                            rows = tuple(a[:, k, j * P:(j + 1) * P] for a in (y_hi, y_lo))
                            mm = three_products(pe, ps[:, :], rows, w["wo", k], k == 0, k == EC - 1)
                    elif m == "k":
                        pe.wait_ge(sems["c_hi"], CC)
                        pe.wait_ge(sems["c_lo"], CC)
                        for name, a, z in (("xwk", 0, MAIN), ("xwk_dca", MAIN, S)):
                            for k in range(CC):
                                wk = tuple(x[:, j * P:(j + 1) * P] for x in w[name, k])
                                ck = (c_hi[:, k, a:z], c_lo[:, k, a:z])
                                mm = three_products(pe, ps[:, a:z], wk, ck, k == 0, k == CC - 1)
                    elif m == "v":
                        tile, name = (j, "xwv") if j < TT else (TT - 1, "xwv_dca")
                        for k in range(CC):
                            ck = tuple(a[:, k, tile * P:(tile + 1) * P] for a in (c_hi, c_lo))
                            mm = three_products(pe, ps[:, :], ck, w[name, k], k == 0, k == CC - 1)
                    elif m == "turn":
                        pe.wait_ge(sems["x1_done"], TT)
                        for n in range(TT):
                            mm = pe.transpose(ps[:, n * P:(n + 1) * P], x_in[:, n, j * P:(j + 1) * P], ident[:, :])
                    elif m == "q":
                        for k in range(EC):
                            if j == 0:
                                pe.wait_ge(sems["y_lo_done"], k + 1)
                            wk = tuple(x[:, j * P:(j + 1) * P] for x in w["xwq", k])
                            mm = three_products(pe, ps[:, :], wk, (y_hi[:, k, :], y_lo[:, k, :]),
                                                k == 0, k == EC - 1)
                    else:
                        n = heads.index((m[0], j))
                        pe.wait_ge(sems["squares_done"], n + 1)
                        mm = pe.matmul(ps[:, :], head_mean[:, :], squares[:, n % DEPTH, :], start=True, stop=True)
                    mm.then_inc(bank.full(key), 1)

        loop_over_batch(nc, ctx, names, build)



def ffn(nc, t, scratch):
    with ExitStack() as ctx:
        wo = split_weights(nc, ctx, "w5o", [(("xwo", k), t["xwo"][k * P:(k + 1) * P, :]) for k in range(EC)], E)
        gates = [((m, k), t[m][k * P:(k + 1) * P, :]) for m in ("wg", "wu") for k in range(EC)]
        w_up = split_weights(nc, ctx, "w5g", gates, HID, integers=True)
        w_down = split_weights(nc, ctx, "w5d", [(("wd", c), t["wd"][c * P:(c + 1) * P, :]) for c in range(FC)], E,
                               integers=True)
        sb = lambda n, shape, dt=F32: ctx.enter_context(nc.sbuf_tensor(f"f_{n}", shape, dt))
        a_raw = sb("a_raw", [P, EC, S])
        y_hi, y_lo = sb("y_hi", [P, EC, S], F32R), sb("y_lo", [P, EC, S], F32R)
        x_in = sb("x_in", [P, TT, E])
        silu = sb("silu", [P, S])
        hidden = sb("hidden", [P, 2, S])
        h_hi, h_lo = sb("h_hi", [P, 2, S], F32R), sb("h_lo", [P, 2, S], F32R)
        bo, s_down = sb("bo", [P, E]), sb("s_down", [P, E])
        s_up = sb("s_up", [P, 2, FC])
        stats, moments = sb("stats", [P, TT, 6]), sb("moments", [P, TT, 2])
        log_var, rstd, eps = sb("log_var", [P, TT]), sb("rstd", [P, TT]), sb("eps", [P, 1])
        ident = sb("ident", [P, P])
        ps_y = [ctx.enter_context(nc.psum_tensor(f"ps5_y{n}", [P, S], F32)) for n in range(TT)]
        ps_h = [ctx.enter_context(nc.psum_tensor(f"ps5_h{n}", [P, S], F32)) for n in range(4)]
        const_in = ctx.enter_context(nc.semaphore("f_const_in"))
        with nc.Block() as block:
            @block.sync
            def _(sp):
                sp.dma_start(ident[:, :], t["ident"]).then_inc(const_in, DMA)
                sp.dma_start(bo[:, :], t["xbo"].partition_broadcast(P)).then_inc(const_in, DMA)
                sp.dma_start(s_down[:, :], t["sd"].partition_broadcast(P)).then_inc(const_in, DMA)
                sp.dma_start(s_up[:, :, :], t["s_up"]).then_inc(const_in, DMA)
                sp.wait_ge(const_in, 4 * DMA)

            @block.vector
            def _(dve):
                dve.memset(eps[:, :], LN_EPS)

        order = [("turn", k) for k in range(EC)] + [(m, c) for c in range(FC) for m in ("wg", "wu")]
        names = ["a_in", "x_in", "biased", "a_hi", "a_lo", "wo_full", "z_done", "stats_done", "moments_done",
                 "log_done", "rstd_done", "x2_done", "y_hi_done", "y_lo_done", "silu_done", "hidden_done",
                 "h_hi_done", "h_lo_done", "down_done", "y_full", "scaled_done", "out_done",
                 "out_stored"] + Banks.names(4)

        def build(block, b, sems):
            bank = Banks(order, ps_h, sems)

            def full(eng, key):
                eng.wait_ge(bank.full(key), bank.round(key) + 1)

            @block.sync
            def _(sp):
                sp.dma_start(a_raw[:, :, :], scratch["ctx"][bass.ds(b, 1)].rearrange("a k p n -> p (a k) n")
                             ).then_inc(sems["a_in"], DMA)
                sp.dma_start(x_in[:, :, :], scratch["x1"][bass.ds(b, 1)].rearrange("a (t p) e -> p (a t) e", p=P)
                             ).then_inc(sems["x_in"], DMA)
                sp.wait_ge(sems["out_done"], TT)
                sp.dma_start(t["out"][bass.ds(b, 1)].rearrange("a (t p) e -> p (a t) e", p=P), x_in[:, :, :]
                             ).then_inc(sems["out_stored"], DMA)
                sp.wait_ge(sems["out_stored"], DMA)

            @block.gpsimd
            def _(pool):
                pool.wait_ge(sems["x_in"], DMA)
                for n in range(TT):
                    pool.tensor_tensor(x_in[:, n, :], x_in[:, n, :], bo[:, :], ALU.add).then_inc(sems["biased"], 1)

            @block.scalar
            def _(act):
                act.wait_ge(sems["a_in"], DMA)
                for k in range(EC):
                    act.activation(y_hi[:, k, :], a_raw[:, k, :], ACT.Copy).then_inc(sems["a_hi"], 1)

                def inverse(turn):
                    act.wait_ge(sems["moments_done"], TT * (turn + 1))
                    act.activation(log_var[:, :], moments[:, :, 1], ACT.Ln, bias=eps[:, 0:1]
                                   ).then_inc(sems["log_done"], 1)
                    act.wait_ge(sems["log_done"], turn + 1)
                    act.activation(rstd[:, :], log_var[:, :], ACT.Exp, scale=-0.5).then_inc(sems["rstd_done"], 1)

                inverse(0)
                for k in range(EC):
                    full(act, ("turn", k))
                    act.activation(y_hi[:, k, :], bank.tile(("turn", k))[:, :], ACT.Copy).then_inc(sems["y_hi_done"], 1)
                for c in range(FC):
                    full(act, ("wg", c))
                    if c:
                        act.wait_ge(sems["hidden_done"], c)
                    act.activation(silu[:, :], bank.tile(("wg", c))[:, :], ACT.Silu, scale=s_up[:, 0, c:c + 1]
                                   ).then_inc(sems["silu_done"], 1)
                    act.wait_ge(sems["hidden_done"], c + 1)
                    if c >= 2:
                        act.wait_ge(sems["down_done"], c - 1)
                    act.activation(h_hi[:, c % 2, :], hidden[:, c % 2, :], ACT.Copy).then_inc(sems["h_hi_done"], 1)
                inverse(1)

            @block.vector
            def _(dve):
                dve.wait_ge(sems["a_in"], DMA)
                for k in range(EC):
                    dve.wait_ge(sems["a_hi"], k + 1)
                    dve.tensor_tensor(y_lo[:, k, :], a_raw[:, k, :], y_hi[:, k, :].bitcast(F32), ALU.subtract
                                      ).then_inc(sems["a_lo"], 1)
                z = a_raw
                dve.wait_ge(sems["a_lo"], EC)

                def norm(turn, n):
                    dve.wait_ge(sems["z_done"], TT * turn + n + 1)
                    dve.bn_stats(stats[:, n, :], z[:, n, :]).then_inc(sems["stats_done"], 1)
                    dve.wait_ge(sems["stats_done"], TT * turn + n + 1)
                    dve.bn_aggr(moments[:, n, :], stats[:, n, :]).then_inc(sems["moments_done"], 1)

                def scale(turn, done):
                    dve.wait_ge(sems["moments_done"], TT * (turn + 1))
                    dve.wait_ge(sems["rstd_done"], turn + 1)
                    for n in range(TT):
                        dve.tensor_scalar(x_in[:, n, :], z[:, n, :], moments[:, n, 0:1], rstd[:, n:n + 1],
                                          ALU.subtract, ALU.mult).then_inc(done, 1)

                for n in range(TT):
                    dve.wait_ge(sems["wo_full"], n + 1)
                    dve.wait_ge(sems["biased"], n + 1)
                    dve.tensor_tensor(z[:, n, :], ps_y[n][:, :], x_in[:, n, :], ALU.add).then_inc(sems["z_done"], 1)
                    norm(0, n)
                scale(0, sems["x2_done"])
                for k in range(EC):
                    full(dve, ("turn", k))
                    dve.wait_ge(sems["y_hi_done"], k + 1)
                    dve.tensor_tensor(y_lo[:, k, :], bank.tile(("turn", k))[:, :], y_hi[:, k, :].bitcast(F32),
                                      ALU.subtract).then_inc(sems["y_lo_done"], 1)
                for c in range(FC):
                    full(dve, ("wu", c))
                    dve.wait_ge(sems["silu_done"], c + 1)
                    if c >= 2:
                        dve.wait_ge(sems["h_hi_done"], c - 1)
                        dve.wait_ge(sems["h_lo_done"], c - 1)
                    dve.scalar_tensor_tensor(hidden[:, c % 2, :], bank.tile(("wu", c))[:, :], s_up[:, 1, c:c + 1],
                                             silu[:, :], ALU.mult, ALU.mult).then_inc(sems["hidden_done"], 1)
                    dve.wait_ge(sems["hidden_done"], c + 1)
                    dve.wait_ge(sems["h_hi_done"], c + 1)
                    dve.tensor_tensor(h_lo[:, c % 2, :], hidden[:, c % 2, :], h_hi[:, c % 2, :].bitcast(F32),
                                      ALU.subtract).then_inc(sems["h_lo_done"], 1)
                dve.wait_ge(sems["x2_done"], TT)
                for n in range(TT):
                    dve.wait_ge(sems["y_full"], n + 1)
                    dve.tensor_tensor(z[:, n, :], ps_y[n][:, :], s_down[:, :], ALU.mult).then_inc(sems["scaled_done"], 1)
                    dve.wait_ge(sems["scaled_done"], n + 1)
                    dve.tensor_tensor(z[:, n, :], z[:, n, :], x_in[:, n, :], ALU.add).then_inc(sems["z_done"], 1)
                    norm(1, n)
                scale(1, sems["out_done"])

            @block.tensor
            def _(pe):
                for n in range(TT):
                    for k in range(EC):
                        pe.wait_ge(sems["a_hi"], k + 1)
                        pe.wait_ge(sems["a_lo"], k + 1)
                        rows = tuple(a[:, k, n * P:(n + 1) * P] for a in (y_hi, y_lo))
                        mm = three_products(pe, ps_y[n][:, :], rows, wo["xwo", k], k == 0, k == EC - 1)
                    mm.then_inc(sems["wo_full"], 1)
                pe.wait_ge(sems["x2_done"], TT)
                for k in range(EC):
                    ps = bank.tile(("turn", k))
                    for n in range(TT):
                        mm = pe.transpose(ps[:, n * P:(n + 1) * P], x_in[:, n, k * P:(k + 1) * P], ident[:, :])
                    mm.then_inc(bank.full(("turn", k)), 1)

                def down(c):
                    pe.wait_ge(sems["h_hi_done"], c + 1)
                    pe.wait_ge(sems["h_lo_done"], c + 1)
                    if c == 0:
                        pe.wait_ge(sems["z_done"], TT)
                    for n in range(TT):
                        rows = (h_hi[:, c % 2, n * P:(n + 1) * P], h_lo[:, c % 2, n * P:(n + 1) * P])
                        mm = three_products(pe, ps_y[n][:, :], rows, w_down["wd", c], c == 0, c == FC - 1)
                        if c == FC - 1:
                            mm.then_inc(sems["y_full"], 1)
                    if c < FC - 1:
                        mm.then_inc(sems["down_done"], 1)

                for c in range(FC):
                    for i, m in enumerate(("wg", "wu")):
                        key = (m, c)
                        use = bank.at[key]
                        if use < 8:
                            if use >= 4:
                                pe.wait_ge(sems["y_lo_done"], use - 3)
                        if c >= 2:
                            pe.wait_ge(sems["silu_done"] if i == 0 else sems["hidden_done"], c - 1)
                        for k in range(EC):
                            pe.wait_ge(sems["y_hi_done"], k + 1)
                            pe.wait_ge(sems["y_lo_done"], k + 1)
                            wk = tuple(a[:, c * P:(c + 1) * P] for a in w_up[m, k])
                            mm = three_products(pe, bank.tile(key)[:, :], wk, (y_hi[:, k, :], y_lo[:, k, :]),
                                                k == 0, k == EC - 1)
                        mm.then_inc(bank.full(key), 1)
                    if c:
                        down(c - 1)
                down(FC - 1)

        loop_over_batch(nc, ctx, names, build)


def build(nc, t):
    scratch = {}
    for name, shape in (("q", (B, 2, 2, 2 * P, S)), ("k", (B, 2, 2, 2 * P, S)), ("v", (B, P, TT * E)),
                        ("attn", (B, EC, P, S)), ("x1", (B, S, E)), ("cq", (B, 2, EC, P, S)),
                        ("ck", (B, 2, EC, P, S)), ("cv", (B, P, (TT + 1) * E)), ("ctx", (B, EC, P, S))):
        scratch[name] = nc.dram_tensor(f"scratch_{name}", shape, F32).ap()
    self_projections(nc, t, scratch)
    attention(nc, t, scratch, "self")
    middle(nc, t, scratch)
    attention(nc, t, scratch, "cross")
    ffn(nc, t, scratch)



def rope_order(np):
    f = np.arange(E).reshape(2, 2, G, 2, PAIRS, 2)
    return f.transpose(0, 5, 1, 3, 2, 4).reshape(E)


def kernel(**inputs):
    import numpy as np
    import concourse.bacc as bacc
    from concourse.bass_utils import run_bass_kernel_spmd

    a = {k: np.asarray(v) for k, v in inputs.items()}
    order = rope_order(np)
    kv = np.concatenate([a["L0_xattn_Wk"], a["L0_xattn_Wv"]], -1).reshape(CD, H, 2, HW)
    bkv = np.concatenate([a["L0_xattn_bk"], a["L0_xattn_bv"]]).reshape(H, 2, HW)
    head_biases = (a["L0_xattn_bq"], bkv[:, 0].reshape(E), a["L0_xattn_bkv_dca"][:E])
    arrays = {
        "x": a["x"], "xT": a["x"].transpose(0, 2, 1), "cT": a["ctx_1024"].transpose(0, 2, 1),
        "wq": a["L0_attn_Wq"].T[:, order], "wk": a["L0_attn_Wk"].T[:, order],
        "wv": a["L0_attn_Wv"].T, "wo": a["L0_attn_Wo"].T,
        "xwq": a["L0_xattn_Wq"], "xwk": kv[:, :, 0].reshape(CD, E), "xwv": kv[:, :, 1].reshape(CD, E),
        "xwkv_dca": a["L0_xattn_Wkv_dca"], "xwo": a["L0_xattn_Wo"],
        "wg": a["L0_ffn_wq_gate"].T, "wu": a["L0_ffn_wq_up"].T, "wd": a["L0_ffn_wq_down"].T,
        "sd": a["L0_ffn_s_down"], "xbv": bkv[:, 1].reshape(E), "xbo": a["L0_xattn_bo"],
        "xbkv_dca": a["L0_xattn_bkv_dca"],
        "s_up": np.stack([a["L0_ffn_" + n].reshape(FC, P).T for n in ("s_gate", "s_up")], 1),
        "gamma": np.tile(a["L0_attn_gamma"], G)[:, None],
        "head_bias": np.stack([v.reshape(EC, P).T for v in head_biases], 1),
        "head_affine": np.stack([np.tile(a["L0_xattn_" + n], G) for n in
                                 ("qn_w", "qn_b", "kn_w", "kn_b", "kn_dca_w", "kn_dca_b")], 1),
    }
    for n in ("lambda_q1", "lambda_k1", "lambda_q2", "lambda_k2"):
        arrays[n] = a["L0_attn_" + n]

    f = np.float32
    angle = (f(1.0) / np.power(f(2500.0), np.linspace(0.0, 1.0, PAIRS, dtype=f))).astype(f)
    phase = (np.arange(S, dtype=f)[None, :] * angle[:, None]).astype(f).astype(np.float64)
    arrays["trig"] = np.tile(np.stack([np.cos(phase), np.sin(phase)], 1), (P // PAIRS, 1, 1)).astype(f)
    arrays["ident"] = np.eye(P, dtype=f)
    arrays["head_mean"] = np.kron(np.eye(G), np.full((HW, HW), 1.0 / HW)).astype(f)
    arrays["centring"] = arrays["ident"] - arrays["head_mean"]
    main = (np.arange(S) < MAIN).astype(f)
    arrays["key_rows"] = np.stack([main, main, 1 - main, 1 - main])
    arrays["masks"] = np.stack([main[-P:], 1 - main[-P:]], 1)

    nc = bacc.Bacc("TRN2", target_bir_lowering=False, num_devices=1)
    arrays = {n: np.ascontiguousarray(v) for n, v in arrays.items()}
    t = {n: nc.dram_tensor(f"in_{n}", v.shape, mybir.dt.from_np(v.dtype), kind="ExternalInput").ap()
         for n, v in arrays.items()}
    t["out"] = nc.dram_tensor("result", (B, S, E), F32, kind="ExternalOutput").ap()
    build(nc, t)
    r = run_bass_kernel_spmd(nc, [{f"in_{n}": v for n, v in arrays.items()}], core_ids=[0])
    return r.results[0]["result"]
```

```python
from contextlib import ExitStack

import concourse.bass as bass
from concourse import mybir

F32 = mybir.dt.float32
F32R = mybir.dt.float32r
I32 = mybir.dt.int32
ALU = mybir.AluOpType
ACT = mybir.ActivationFunctionType
AX_X = mybir.AxisListType.X
ENGINES = [mybir.EngineType.SP, mybir.EngineType.DVE, mybir.EngineType.Activation,
           mybir.EngineType.Pool, mybir.EngineType.PE]

P = 128
B, S, E = 4, 512, 512
H, HW = 16, 32
HD = HW // 2
PAIRS = HD // 2
CD, DCA = 256, 16
MAIN = S - DCA
HID = 1408
TT = S // P
EC = E // P
CC = CD // P
FC = HID // P
G = P // HW
ZERO_POINT = 128.0
LAMBDA_INIT = 0.8 - 0.6 * 2.718281828459045 ** (-0.3 * 12)
RMS_EPS, LN_EPS, HEAD_EPS = 1e-05, 1e-05, 1e-06
BATCHES = 2
LOOP_SEMS = 180
DMA = 16


LN_AND_EXP = "natural_log_exp_and_others"


def loop_over_batch(nc, ctx, names, build, batches=1):
    sems = {n: ctx.enter_context(nc.semaphore(n, num=LOOP_SEMS + i)) for i, n in enumerate(names)}
    with nc.Fori(0, B // batches) as b:
        with nc.Block() as block:
            build(block, b, sems)
        nc.multi_engine_barrier(ENGINES, sems_to_clear=range(LOOP_SEMS, LOOP_SEMS + len(names)))


def batch_of(tensor, b, batch):
    rest = " ".join("defg"[:len(tensor.shape) - 1])
    return tensor.rearrange(f"(i j) {rest} -> i j {rest}", j=BATCHES)[bass.ds(b, 1), batch]


def own_sems(sems, own, batch):
    return {**sems, **{n: sems[f"{n}_{batch}"] for n in own}}


class Banks:

    def __init__(self, order, tiles, sems):
        self.at = {key: i for i, key in enumerate(order)}
        self.tiles, self.sems = tiles, sems

    @staticmethod
    def names(count):
        return [f"bank_full{n}" for n in range(count)]

    def tile(self, key):
        return self.tiles[self.at[key] % len(self.tiles)]

    def full(self, key):
        return self.sems[f"bank_full{self.at[key] % len(self.tiles)}"]

    def round(self, key):
        return self.at[key] // len(self.tiles)


THREE = ((0, 0), (0, 1), (1, 0))
STATIONARY_WHOLE, MOVING_WHOLE = ((0, 0), (0, 1)), ((0, 0), (1, 0))


def products_of_parts(pe, out, stationary, moving, first, last, terms=THREE):
    for n, (i, j) in enumerate(terms):
        mm = pe.matmul(out, stationary[i], moving[j], start=first and n == 0, stop=last and n == len(terms) - 1)
    return mm


def split_weights(nc, ctx, name, groups, centre=(), square_sum=None):
    SLOTS = 6
    pieces, where = [], {}
    for g, (width, integers, sources) in enumerate(groups):
        hi = ctx.enter_context(nc.sbuf_tensor(f"{name}_hi{g}", [P, width * len(sources)], F32R))
        lo = ctx.enter_context(nc.sbuf_tensor(f"{name}_lo{g}", [P, width * len(sources)], F32R))
        for n, (piece, src) in enumerate(sources):
            where[piece] = (hi[:, n * width:(n + 1) * width], lo[:, n * width:(n + 1) * width])
            pieces.append((piece, src, width, integers))
    centred_pieces = [p for p, *_ in pieces if p in centre]
    widest = max(width for width, *_ in groups)
    with ExitStack() as inner:
        buffer = inner.enter_context(nc.sbuf_tensor(f"{name}_raw", [P, SLOTS, widest], F32))
        mean = inner.enter_context(nc.sbuf_tensor(f"{name}_mean", [P, SLOTS, widest // HW], F32))
        raw_in = [inner.enter_context(nc.semaphore(f"{name}_raw_in{n}")) for n in range(SLOTS)]
        hi_done = inner.enter_context(nc.semaphore(f"{name}_hi_done"))
        lo_done = inner.enter_context(nc.semaphore(f"{name}_lo_done"))
        centred = inner.enter_context(nc.semaphore(f"{name}_centred"))

        def raw(n):
            tile = buffer[:, n % SLOTS, 0:pieces[n][2]]
            return tile.bitcast(I32) if pieces[n][3] else tile

        def centred_before(eng, piece):
            if piece in centre:
                eng.wait_ge(centred, 2 * (1 + centred_pieces.index(piece)))

        def lo_part(eng, n):
            piece, _, _, integers = pieces[n]
            hi, lo = where[piece]
            eng.wait_ge(raw_in[n % SLOTS], DMA * (n // SLOTS + 1))
            centred_before(eng, piece)
            eng.wait_ge(hi_done, n + 1)
            if integers:
                eng.scalar_tensor_tensor(lo, raw(n), -ZERO_POINT, hi.bitcast(F32), ALU.add, ALU.subtract
                                         ).then_inc(lo_done, 1)
            else:
                eng.tensor_tensor(lo, raw(n), hi.bitcast(F32), ALU.subtract).then_inc(lo_done, 1)

        with nc.Block() as block:
            @block.sync
            def _(sp):
                for n, (_, src, *_) in enumerate(pieces):
                    if n >= SLOTS:
                        sp.wait_ge(lo_done, n - SLOTS + 1)
                    sp.dma_start(raw(n), src).then_inc(raw_in[n % SLOTS], DMA)

            @block.scalar
            def _(act):
                for n, (piece, _, _, integers) in enumerate(pieces):
                    centred_before(act, piece)
                    act.wait_ge(raw_in[n % SLOTS], DMA * (n // SLOTS + 1))
                    if integers:
                        act.activation(where[piece][0], raw(n), ACT.Copy, bias=-ZERO_POINT).then_inc(hi_done, 1)
                    else:
                        act.activation(where[piece][0], raw(n), ACT.Copy).then_inc(hi_done, 1)

            @block.tensor
            def _(pe):
                blocks = [(n, c) for n, (_, _, width, integers) in enumerate(pieces) if integers
                          for c in range(0, width, P)] if square_sum is not None else []
                for i, (n, c) in enumerate(blocks):
                    pe.wait_ge(lo_done, n + 1)
                    lo = where[pieces[n][0]][1][:, c:c + P]
                    pe.matmul(square_sum, lo, lo, start=i == 0, stop=i == len(blocks) - 1)

            @block.gpsimd
            def _(pool):
                if centre:
                    for n in range(len(pieces)):
                        lo_part(pool, n)

            @block.vector
            def _(dve):
                for n, (piece, _, width, _) in enumerate(pieces):
                    if not centre:
                        lo_part(dve, n)
                    if piece in centre:
                        steps = 2 * centred_pieces.index(piece)
                        dve.wait_ge(raw_in[n % SLOTS], DMA * (n // SLOTS + 1))
                        by_head = raw(n).rearrange("p (h d) -> p h d", d=HW)
                        dve.tensor_reduce(mean[:, n % SLOTS, 0:width // HW], by_head, AX_X, ALU.add
                                          ).then_inc(centred, 1)
                        dve.wait_ge(centred, steps + 1)
                        dve.scalar_tensor_tensor(
                            by_head, mean[:, n % SLOTS, 0:width // HW].unsqueeze(2)
                            .broadcast_to([P, width // HW, HW]),
                            -1.0 / HW, by_head, ALU.mult, ALU.add).then_inc(centred, 1)
    return where



def self_projections(nc, t, scratch):
    with ExitStack() as ctx:
        sources = [((m, k), t[m][k * P:(k + 1) * P, :]) for m in ("wq", "wk", "wv") for k in range(EC)]
        w = split_weights(nc, ctx, "w1", [(E, False, sources)])
        sb = lambda n, shape, dt=F32: ctx.enter_context(nc.sbuf_tensor(n, shape, dt))
        trig = sb("trig", [P, 2, S])
        each = lambda n, shape, dt=F32: [sb(f"{n}{batch}", shape, dt) for batch in range(BATCHES)]
        x_raws = each("x_raw", [P, EC, S])
        x_his, x_los = each("x_hi", [P, EC, S], F32R), each("x_lo", [P, EC, S], F32R)
        vs = each("v_out", [P, TT, E])
        products = sb("rope_products", [P, 2, 4, S])
        rotated = sb("rotated", [P, 2, 2 * S])
        parts = sb("parts", [P, 2, 2, 2 * S])
        psum = [ctx.enter_context(nc.psum_tensor(f"ps1_{n}", [P, S], F32)) for n in range(8)]
        trig_in = ctx.enter_context(nc.semaphore("trig_in"))
        with nc.Block() as block:
            @block.sync
            def _(sp):
                sp.dma_start(trig[:, :, :], t["trig"]).then_inc(trig_in, DMA)
                sp.wait_ge(trig_in, DMA)

        turns = [("q", 0), ("k", 0), ("q", 1), ("k", 1)]
        keys = [(m, j, e) for m, j in turns for e in range(2)] + [("v", n, 0) for n in range(TT)]
        order = [(batch, *key) for batch in range(BATCHES) for key in keys]
        own = [f"x_in{k}" for k in range(EC)] + ["x_hi_done", "x_lo_done", "v_done", "v_out_done"]
        names = [f"{n}_{batch}" for batch in range(BATCHES) for n in own]
        names += ["products_ready", "rotated_ready", "hi_done", "lo_done", "parts_out0", "parts_out1"] + Banks.names(8)

        def build(block, b, all_sems):
            bank = Banks(order, psum, all_sems)
            for batch in range(BATCHES):
                loads(block, b, all_sems, batch)
            for batch in range(BATCHES):
                projections(block, b, all_sems, batch, bank)

            @block.sync
            def _(sp):
                for batch in range(BATCHES):
                    sp.wait_ge(all_sems[f"v_out_done_{batch}"], DMA)
                for n in range(2):
                    sp.wait_ge(all_sems[f"parts_out{n}"], BATCHES * len(turns) // 2 * DMA)

        def loads(block, b, all_sems, batch):
            sems = own_sems(all_sems, own, batch)
            x_raw, x_hi, x_lo = x_raws[batch], x_his[batch], x_los[batch]

            @block.sync
            def _(sp):
                for k in range(EC):
                    sp.dma_start(x_raw[:, k, :], batch_of(t["xT"], b, batch)[:, k * P:(k + 1) * P, :]
                                 .rearrange("a p n -> p (a n)")).then_inc(sems[f"x_in{k}"], DMA)

            @block.scalar
            def _(act):
                for k in range(EC):
                    act.wait_ge(sems[f"x_in{k}"], DMA)
                    act.activation(x_hi[:, k, :], x_raw[:, k, :], ACT.Copy).then_inc(sems["x_hi_done"], 1)

            @block.vector
            def _(dve):
                for k in range(EC):
                    dve.wait_ge(sems["x_hi_done"], k + 1)
                    dve.wait_ge(sems[f"x_in{k}"], DMA)
                    dve.tensor_tensor(x_lo[:, k, :], x_raw[:, k, :], x_hi[:, k, :].bitcast(F32),
                                      ALU.subtract).then_inc(sems["x_lo_done"], 1)

        def bank_free(pe, all_sems, bank, batch, key):
            if bank.round((batch, *key)):
                former, m, j, _ = order[bank.at[(batch, *key)] - 8]
                if m == "v":
                    pe.wait_ge(all_sems[f"v_done_{former}"], j + 1)
                else:
                    pe.wait_ge(all_sems["products_ready"], former * len(turns) + turns.index((m, j)) + 1)

        def projections(block, b, all_sems, batch, bank):
            sems = own_sems(all_sems, own, batch)
            x_hi, x_lo, v = x_his[batch], x_los[batch], vs[batch]
            before = batch * len(turns)
            result = lambda key: bank.tile((batch, *key))

            def full(eng, key):
                eng.wait_ge(bank.full((batch, *key)), bank.round((batch, *key)) + 1)

            @block.sync
            def _(sp):
                for n, (m, j) in enumerate(turns):
                    sp.wait_ge(sems["lo_done"], before + n + 1)
                    sp.dma_start(batch_of(scratch[m], b, batch)[:, :, j].rearrange("a k (p e) n -> p (a k) e n", e=2),
                                 parts[:, n % 2].rearrange("p k (e n) -> p k e n", e=2)
                                 ).then_inc(sems[f"parts_out{n % 2}"], DMA)
                sp.wait_ge(sems["v_done"], TT)
                sp.dma_start(batch_of(scratch["v"], b, batch).rearrange("a p n -> p (a n)"),
                             v[:, :, :].rearrange("p t n -> p (t n)")).then_inc(sems["v_out_done"], DMA)

            @block.scalar
            def _(act):
                for n in range(before, before + len(turns)):
                    act.wait_ge(sems["rotated_ready"], n + 1)
                    if n >= 2:
                        act.wait_ge(sems[f"parts_out{n % 2}"], DMA * (n // 2))
                    act.activation(parts[:, n % 2, 0, :].bitcast(F32R), rotated[:, n % 2, :],
                                   ACT.Copy).then_inc(sems["hi_done"], 1)
                for n in range(TT):
                    full(act, ("v", n, 0))
                    act.activation(v[:, n, :], result(("v", n, 0))[:, :], ACT.Copy).then_inc(sems["v_done"], 1)

            @block.gpsimd
            def _(pool):
                for n in range(before, before + len(turns)):
                    pool.wait_ge(sems["products_ready"], n + 1)
                    if n >= 2:
                        pool.wait_ge(sems["hi_done"], n - 1)
                    pool.tensor_tensor(rotated[:, n % 2, 0:S], products[:, n % 2, 0, :], products[:, n % 2, 1, :],
                                       ALU.subtract)
                    pool.tensor_tensor(rotated[:, n % 2, S:2 * S], products[:, n % 2, 2, :],
                                       products[:, n % 2, 3, :], ALU.add).then_inc(sems["rotated_ready"], 1)
                    pool.wait_ge(sems["hi_done"], n + 1)
                    pool.wait_ge(sems["rotated_ready"], n + 1)
                    pool.tensor_tensor(parts[:, n % 2, 1, :].bitcast(F32R), rotated[:, n % 2, :],
                                       parts[:, n % 2, 0, :], ALU.subtract).then_inc(sems["lo_done"], 1)

            @block.vector
            def _(dve):
                for turn, (m, j) in enumerate(turns):
                    even, odd, n = (m, j, 0), (m, j, 1), before + turn
                    if n >= 2:
                        dve.wait_ge(sems["rotated_ready"], n - 1)
                    full(dve, even)
                    dve.tensor_tensor(products[:, n % 2, 0, :], result(even)[:, :], trig[:, 0, :], ALU.mult)
                    dve.tensor_tensor(products[:, n % 2, 2, :], result(even)[:, :], trig[:, 1, :], ALU.mult)
                    full(dve, odd)
                    dve.tensor_tensor(products[:, n % 2, 1, :], result(odd)[:, :], trig[:, 1, :], ALU.mult)
                    dve.tensor_tensor(products[:, n % 2, 3, :], result(odd)[:, :], trig[:, 0, :],
                                      ALU.mult).then_inc(sems["products_ready"], 1)

            @block.tensor
            def _(pe):
                for key in keys:
                    m, j, e = key
                    bank_free(pe, all_sems, bank, batch, key)
                    for k in range(EC):
                        pe.wait_ge(sems["x_hi_done"], k + 1)
                        pe.wait_ge(sems["x_lo_done"], k + 1)
                        xk = (x_hi[:, k, :], x_lo[:, k, :])
                        if m == "v":
                            xk = tuple(a[:, j * P:(j + 1) * P] for a in xk)
                            mm = products_of_parts(pe, result(key)[:, :], xk, w["wv", k], k == 0, k == EC - 1)
                        else:
                            c = (2 * j + e) * P
                            wk = tuple(a[:, c:c + P] for a in w["w" + m, k])
                            mm = products_of_parts(pe, result(key)[:, :], wk, xk, k == 0, k == EC - 1)
                    mm.then_inc(bank.full((batch, *key)), 1)

        loop_over_batch(nc, ctx, names, build, BATCHES)



def attention(nc, t, scratch, kind):
    cross = kind == "cross"
    NHB = H // G if cross else 2 * H // G
    NH = BATCHES * NHB
    RW = HW if cross else HD
    SCALE = float(RW) ** -0.5
    BIAS = 96
    ROWS = BIAS + (4 if cross else 2)
    NK = MAIN if cross else S
    NM = 2 * 16 if cross else 16
    STEPS = NH * TT
    SLOTS, PB = 4, 4
    with ExitStack() as ctx:
        sb = lambda n, shape, dt=F32: ctx.enter_context(nc.sbuf_tensor(f"{kind}_{n}", shape, dt))
        q_stack = sb("q_stack", [P, SLOTS, 4, S], F32R)
        k_stack = sb("k_stack", [P, SLOTS, 4, S], F32R)
        probs = sb("probs", [P, PB, 4, S])
        partial = sb("partial", [P, 2, 4, S])
        NV = TT + cross
        v = sb("v", [P, BATCHES, NV, E])
        ones = sb("ones", [P, HW])
        ident = sb("ident", [P, P])
        head_mean = sb("head_mean", [P, P])
        key_rows = sb("key_rows", [P, S])
        neg_max = sb("neg_max", [P, 2, NM])
        m_hi, m_lo = sb("m_hi", [P, 2, P]), sb("m_lo", [P, 2, P])
        log_sum = sb("log_sum", [P, S])
        inv_sum = sb("inv_sum", [P, S])
        first = sb("first", [P, S])
        out = sb("out", [P, 2, S])
        lam = sb("lam", [P, 4, HD])
        lam_sums = sb("lam_sums", [P, 2])
        lam_work = sb("lam_work", [P, 3, HD])
        neg_lam = sb("neg_lam", [P, 1])
        gamma = sb("gamma", [P, 2])
        diff = sb("diff", [P, 2, S])
        mean_sq = sb("mean_sq", [P, 2, S])
        ps_s = [ctx.enter_context(nc.psum_tensor(f"{kind}_ps_s{n}", [P, S], F32)) for n in range(2)]
        ps_t = [ctx.enter_context(nc.psum_tensor(f"{kind}_ps_t{n}", [P, 2 * S], F32)) for n in range(2)]
        ps_o = ctx.enter_context(nc.psum_tensor(f"{kind}_ps_o", [P, S], F32))
        ps_l = ctx.enter_context(nc.psum_tensor(f"{kind}_ps_l", [P, S], F32))

        if cross:
            last_keys = sb("last_keys", [P, 2, HW])
            masks = sb("masks", [P, 2])

        sem = lambda n: ctx.enter_context(nc.semaphore(f"{kind}_{n}"))
        const_in, const_set, lam_in, lam_done = sem("const_in"), sem("const_set"), sem("lam_in"), sem("lam_done")
        with nc.Block() as block:
            @block.sync
            def _(sp):
                sp.dma_start(ident[:, :], t["ident"]).then_inc(const_in, DMA)
                sp.dma_start(head_mean[:, :], t["head_mean"]).then_inc(const_in, DMA)
                if cross:
                    sp.dma_start(key_rows[BIAS:BIAS + 4, :], t["key_rows"]).then_inc(const_in, DMA)
                    sp.dma_start(masks[:, :], t["masks"]).then_inc(const_in, DMA)
                if not cross:
                    for n, name in enumerate(("lambda_q1", "lambda_k1", "lambda_q2", "lambda_k2")):
                        sp.dma_start(lam[:, n, :], t[name].partition_broadcast(P)).then_inc(lam_in, DMA)
                    sp.dma_start(gamma[:, 0:1], t["gamma"]).then_inc(lam_in, DMA)
                sp.wait_ge(const_in, (4 if cross else 2) * DMA)

            @block.gpsimd
            def _(pool):
                if not cross:
                    pool.memset(q_stack[0:BIAS, :, :, :].bitcast(F32), 0.0)

            @block.vector
            def _(dve):
                dve.memset(ones[:, :], 1.0).then_inc(const_set, 1)
                if cross:
                    dve.wait_ge(const_in, 4 * DMA)
                    dve.wait_ge(const_set, 1)
                    dve.tensor_copy(k_stack[BIAS:ROWS, :, :, :].rearrange("p a u n -> p (a u) n"),
                                    key_rows[BIAS:ROWS, :].unsqueeze(1).to_broadcast([ROWS - BIAS, 4 * SLOTS, S]))
                    for n in range(2):
                        dve.tensor_scalar(last_keys[:, n, :], ones[:, :], masks[:, n:n + 1], None, ALU.mult)
                else:
                    dve.memset(k_stack[0:BIAS, :, :, :].bitcast(F32), 0.0)
                    dve.wait_ge(lam_in, 5 * DMA)
                    for n in range(2):
                        dve.tensor_tensor(lam_work[:, n, :], lam[:, 2 * n, :], lam[:, 2 * n + 1, :],
                                          ALU.mult).then_inc(lam_done, 1)
                    dve.wait_ge(lam_done, 2)
                    dve.tensor_reduce(lam_sums[:, :], lam_work[:, 0:2, :], AX_X, ALU.add).then_inc(lam_done, 1)
                    dve.tensor_scalar(gamma[:, 1:2], gamma[:, 0:1], 1.0 - LAMBDA_INIT, None, ALU.mult)
                    dve.wait_ge(lam_done, 4)
                    dve.scalar_tensor_tensor(neg_lam[:, :], lam_work[:, 2, 1:2], -LAMBDA_INIT, lam_work[:, 2, 0:1],
                                             ALU.add, ALU.subtract)

            @block.scalar
            def _(act):
                if not cross:
                    act.wait_ge(const_set, 1)
                    for n in range(SLOTS):
                        act.activation(k_stack[BIAS:ROWS, n, :, :].rearrange("p u n -> p (u n)"),
                                       ones[BIAS:ROWS, 0:1].to_broadcast([ROWS - BIAS, 4 * S]), ACT.Copy)
                    act.wait_ge(lam_done, 3)
                    act.activation(lam_work[:, 2, 0:2], lam_sums[:, :], ACT.Exp).then_inc(lam_done, 1)

        LEAD = 6 * TT + 2
        SHARE = (6, 3, 3, 5)
        stream = []
        for h in range(NH):
            stream += [("scores", h, u, n) for u in range(4) for n in range(TT)]
            stream.insert(len(stream) - (4 * TT - 1 if h else 0), ("maxima", h - 1))
        stream = [key for key in stream if key[1] >= 0] + [("maxima", NH - 1)]
        uses, taken = {-1: stream[:LEAD]}, LEAD
        for st in range(STEPS):
            h, c = divmod(st, TT)
            uses[st] = stream[taken:taken + SHARE[c]]
            taken += SHARE[c]
            if not cross and c == 3 and h % 2 == 0 and h:
                uses[st].append(("rms", h // 2 - 1))
        uses[STEPS] = [] if cross else [("rms", NH // 2 - 1)]
        use_at = {key: i for i, key in enumerate(k for st in range(-1, STEPS + 1) for k in uses[st])}

        products = {st: [] for st in range(STEPS + 3)}
        for h in range(NH):
            for c, st in enumerate((2, 2, 3) if cross else (1, 2, 3)):
                products[TT * h + st].append(("pv", h, c))
            products[TT * h + TT] += [("sum_last", h), ("sum_first", h), ("pv", h, TT - 1)]
            if cross:
                products[TT * h + TT + 1] += [("dca_sum", h), ("dca", h)]
        product_at = {key: i for i, key in enumerate(k for st in range(STEPS + 3) for k in products[st])}
        results = [k for k in product_at if k[0] == "dca" or k[0] == "pv" and k[2] == TT - 1]
        result_at = {key: i for i, key in enumerate(results)}
        sum_of = {key: ("dca_sum" if key[0] == "dca" else "sum_first", key[1]) for key in results}

        names = ["v_in0", "v_in1", *(f"{n}{i}" for n in ("stack_in", "bias_in") for i in range(SLOTS)),
                 "scores_ready", "scores_read", "turned_hi", "shifted_ready",
                 "exp_done", "added", "products_done", "log_done", "inverse_done", "output_read",
                 "diff_done", "squares_done", "rms_log", "rms_done", "out_done",
                 "out_stored0", "out_stored1"]
        NOUTB = NHB if cross else NHB // 2
        NOUT = BATCHES * NOUTB
        assert BATCHES == 2
        NB = 4 if cross else 2

        def build(block, b, sems):
            stack_in = [sems[f"stack_in{n}"] for n in range(SLOTS)]
            bias_in = [sems[f"bias_in{n}"] for n in range(SLOTS)]
            out_stored = [sems[f"out_stored{n}"] for n in range(2)]

            scratch_of = lambda name, batch: batch_of(scratch[name], b, batch)

            @block.sync
            def _(sp):
                def gather(h):
                    if h >= SLOTS:
                        sp.wait_ge(sems["shifted_ready"], 2 * TT * (h - SLOTS + 1))
                    batch, hb = divmod(h, NHB)
                    for m, stack, kinds in (("q", q_stack, (0, 0, 1)), ("k", k_stack, (0, 1, 0))):
                        for term, part in enumerate(kinds):
                            if cross:
                                src = scratch_of("c" + m, batch)[:, part, hb]
                            else:
                                r0 = (hb % 4) * 4 * HD
                                src = scratch_of(m, batch)[:, part, hb // 4, r0:r0 + 4 * HD]
                            sp.dma_start(stack[term * RW:(term + 1) * RW, h % SLOTS, :, :].bitcast(F32),
                                         src.rearrange("a (c r) n -> r (a c) n", c=4)
                                         ).then_inc(stack_in[h % SLOTS], DMA)

                def bias(h):
                    sp.wait_ge(sems["scores_read"], use_at["maxima", h] + 1)
                    for n in range(NB):
                        part = (m_hi, m_lo)[n % 2]
                        sp.dma_start(
                            q_stack[BIAS + n:BIAS + n + 1, h % SLOTS, :, :].bitcast(F32)
                            .rearrange("a u (t n) -> a (u t) n", t=TT),
                            part[16 * (n // 2):16 * (n // 2) + 16, h % 2, :]).then_inc(bias_in[h % SLOTS], DMA)

                def store(g):
                    sp.wait_ge(sems["out_done"], g + 1)
                    batch, gb = divmod(g, NOUTB)
                    sp.dma_start(scratch_of("ctx" if cross else "attn", batch)[:, gb]
                                 .rearrange("a p n -> p (a n)"), out[:, g % 2, :]).then_inc(out_stored[g % 2], DMA)

                gather(0)
                gather(1)
                for batch in range(BATCHES):
                    sp.dma_start(v[:, batch, :, :].rearrange("p t n -> p (t n)"),
                                 scratch_of("cv" if cross else "v", batch).rearrange("a p n -> p (a n)")
                                 ).then_inc(sems[f"v_in{batch}"], DMA)
                gather(2)
                bias(0)
                gather(3)
                bias(1)
                for h in range(NH):
                    if h + SLOTS < NH:
                        gather(h + SLOTS)
                    if h + 2 < NH:
                        bias(h + 2)
                    if not cross and h % 2 and h > 1:
                        store(h // 2 - 1)
                    if cross and h:
                        store(h - 1)
                store(NOUT - 1)
                for n in range(2):
                    sp.wait_ge(out_stored[n], DMA * ((NOUT + 1 - n) // 2))

            @block.tensor
            def _(pe):
                def run(key):
                    i = use_at[key]
                    if i >= 2:
                        pe.wait_ge(sems["scores_read"], i - 1)
                    bank = ps_s[i % 2]
                    if key[0] == "scores":
                        _, h, u, n = key
                        if u == 0 and n == 0:
                            pe.wait_ge(stack_in[h % SLOTS], 6 * DMA * (h // SLOTS + 1))
                        pe.matmul(bank[:, :], q_stack[0:BIAS, h % SLOTS, u, n * P:(n + 1) * P],
                                  k_stack[0:BIAS, h % SLOTS, u, :], start=True, stop=True
                                  ).then_inc(sems["scores_ready"], 1)
                    elif key[0] == "maxima":
                        pe.wait_ge(sems["scores_read"], use_at["scores", key[1], 3, TT - 1] + 1)
                        pe.transpose(bank[0:NM, 0:P], neg_max[:, key[1] % 2, :], ident[:, :]
                                     ).then_inc(sems["scores_ready"], 1)
                    else:
                        pe.wait_ge(sems["squares_done"], key[1] + 1)
                        pe.matmul(bank[:, :], head_mean[:, :], mean_sq[:, 0, :], start=True, stop=True
                                  ).then_inc(sems["scores_ready"], 1)

                def shifted(st, pair):
                    h, c = divmod(st, TT)
                    if c == 0 and pair == 0:
                        pe.wait_ge(bias_in[h % SLOTS], NB * DMA * (h // SLOTS + 1))
                    e = 2 * st + pair
                    if e >= 2:
                        pe.wait_ge(sems["exp_done"], e - 1)
                    for i in range(2):
                        mm = pe.matmul(ps_t[pair][:, i * S:(i + 1) * S],
                                       k_stack[0:ROWS, h % SLOTS, 2 * pair + i, c * P:(c + 1) * P],
                                       q_stack[0:ROWS, h % SLOTS, 2 * pair + i, :], start=True, stop=True)
                    mm.then_inc(sems["shifted_ready"], 1)

                def product(key):
                    kind_of, h = key[:2]
                    batch, hb = divmod(h, NHB)
                    c = key[2] if kind_of == "pv" else TT - 1
                    sums = kind_of in ("sum_last", "sum_first", "dca_sum")
                    begins = kind_of in ("sum_last", "dca_sum", "dca") or kind_of == "pv" and c == 0
                    ends = kind_of in ("sum_first", "dca_sum", "dca") or kind_of == "pv" and c == TT - 1
                    if kind_of == "sum_first":
                        pe.wait_ge(sems["added"], 4 * (h + 1))
                        moving = partial[:, h % 2]
                    else:
                        pe.wait_ge(sems["exp_done"], 2 * (TT * h + c + 1))
                        moving = probs[:, (TT * h + c) % PB]
                    if kind_of == "pv" and hb == 0 and c == 0:
                        pe.wait_ge(sems[f"v_in{batch}"], DMA)
                    if begins:
                        former = result_at[("dca", h) if kind_of in ("dca", "dca_sum") else ("pv", h, TT - 1)]
                        if former:
                            pe.wait_ge(sems["log_done" if sums else "output_read"], former)
                    for u in range(4):
                        rows = slice(HW * u, HW * (u + 1))
                        if sums:
                            w = ones[:, :]
                            if cross and kind_of != "sum_first":
                                w = last_keys[:, 1 if kind_of == "dca_sum" else 0, :]
                        else:
                            head = 4 * hb + u if cross else G * (hb // 2) + u
                            w = v[:, batch, TT if kind_of == "dca" else c, head * HW:(head + 1) * HW]
                        mm = pe.matmul((ps_l if sums else ps_o)[rows, :], w, moving[:, u, :], start=begins, stop=ends)
                    mm.then_inc(sems["products_done"], 1)

                for key in uses[-1]:
                    run(key)
                for st in range(STEPS + 3):
                    early_ones = list(uses[st]) if st < STEPS else []
                    others = ([("shifted", pair) for pair in range(2)] if st < STEPS else []) + products[st]
                    for n, key in enumerate(others):
                        if key[0] == "shifted":
                            shifted(st, key[1])
                        else:
                            product(key)
                        for early_key in early_ones[n * len(early_ones) // len(others):
                                                    (n + 1) * len(early_ones) // len(others)]:
                            run(early_key)
                for key in uses[STEPS]:
                    run(key)

            @block.scalar
            def _(act):
                def inverse(key):
                    n = result_at[key]
                    if n:
                        act.wait_ge(sems["inverse_done"], n)
                    act.wait_ge(sems["products_done"], product_at[sum_of[key]] + 1)
                    act.activation(log_sum[:, :], ps_l[:, :], ACT.Ln).then_inc(sems["log_done"], 1)
                    act.wait_ge(sems["log_done"], n + 1)
                    if n:
                        act.wait_ge(sems["output_read"], n)
                    act.activation(inv_sum[:, :], log_sum[:, :], ACT.Exp, scale=-1.0).then_inc(sems["inverse_done"], 1)

                def rms(g):
                    act.wait_ge(sems["scores_read"], use_at["rms", g] + 1)
                    act.activation(mean_sq[:, 0, :], mean_sq[:, 1, :], ACT.Ln).then_inc(sems["rms_log"], 1)
                    act.wait_ge(sems["rms_log"], g + 1)
                    act.activation(mean_sq[:, 1, :], mean_sq[:, 0, :], ACT.Exp, scale=-0.5).then_inc(sems["rms_done"], 1)

                nc.scalar.preload_act_table_set(LN_AND_EXP)
                for st in range(STEPS + 3):
                    if st < STEPS:
                        for pair in range(2):
                            act.wait_ge(sems["shifted_ready"], 2 * st + pair + 1)
                            if st >= PB and pair == 0:
                                h, c = divmod(st - PB, TT)
                                last = ("dca", h) if cross and c == TT - 1 else ("pv", h, c)
                                act.wait_ge(sems["products_done"], product_at[last] + 1)
                                if c < TT - 1:
                                    act.wait_ge(sems["added"], 4 * h + (2 if c < 2 else 4))
                            act.activation(probs[:, st % PB, 2 * pair:2 * pair + 2, :].rearrange("p u n -> p (u n)"),
                                           ps_t[pair][:, :], ACT.Exp, scale=SCALE).then_inc(sems["exp_done"], 1)
                    for key in products[st]:
                        if key in result_at:
                            inverse(key)
                    if not cross and st % (2 * TT) == TT and 2 * TT < st < STEPS:
                        rms(st // (2 * TT) - 1)
                if not cross:
                    rms(NH // 2 - 1)

            @block.gpsimd
            def _(pool):
                for h in range(NH):
                    for c in (1, 2):
                        for pair in range(2):
                            st = TT * h + c
                            total = partial[:, h % 2, 2 * pair:2 * pair + 2, :]
                            pool.wait_ge(sems["exp_done"], 2 * st + pair + 1)
                            if c == 1 and h >= 2:
                                pool.wait_ge(sems["products_done"], product_at["sum_first", h - 2] + 1)
                            if c == 2:
                                pool.wait_ge(sems["added"], 4 * h + pair + 1)
                            pool.tensor_tensor(total, probs[:, (st - 1) % PB, 2 * pair:2 * pair + 2, :] if c == 1 else total,
                                               probs[:, st % PB, 2 * pair:2 * pair + 2, :], ALU.add
                                               ).then_inc(sems["added"], 1)

            @block.vector
            def _(dve):
                def read(key):
                    i = use_at[key]
                    bank = ps_s[i % 2]
                    dve.wait_ge(sems["scores_ready"], i + 1)
                    if key[0] == "scores":
                        _, h, u, n = key
                        if u == 0 and n == 0 and h >= 2:
                            dve.wait_ge(sems["scores_ready"], use_at["maxima", h - 2] + 1)
                        col = 4 * u + n
                        if cross:
                            dve.tensor_reduce(neg_max[:, h % 2, col:col + 1], bank[:, 0:NK], AX_X, ALU.max,
                                              negate=True)
                            red = dve.tensor_reduce(neg_max[:, h % 2, 16 + col:17 + col], bank[:, NK:S], AX_X,
                                                    ALU.max, negate=True)
                        else:
                            red = dve.tensor_reduce(neg_max[:, h % 2, col:col + 1], bank[:, :], AX_X, ALU.max,
                                                    negate=True)
                        red.then_inc(sems["scores_read"], 1)
                    elif key[0] == "maxima":
                        h = key[1]
                        if h >= 2:
                            dve.wait_ge(bias_in[(h - 2) % SLOTS], NB * DMA * ((h - 2) // SLOTS + 1))
                        dve.tensor_copy(m_hi[0:NM, h % 2, :].bitcast(F32R), bank[0:NM, 0:P]
                                        ).then_inc(sems["turned_hi"], 1)
                        dve.wait_ge(sems["turned_hi"], h + 1)
                        dve.tensor_tensor(m_lo[0:NM, h % 2, :].bitcast(F32R), bank[0:NM, 0:P],
                                          m_hi[0:NM, h % 2, :], ALU.subtract).then_inc(sems["scores_read"], 1)
                    else:
                        g = key[1]
                        if g:
                            dve.wait_ge(sems["out_done"], g)
                        dve.tensor_scalar(mean_sq[:, 1, :], bank[:, :], RMS_EPS, None, ALU.add
                                          ).then_inc(sems["scores_read"], 1)

                def normalise(key):
                    n = result_at[key]
                    dve.wait_ge(sems["inverse_done"], n + 1)
                    dve.wait_ge(sems["products_done"], product_at[key] + 1)
                    if n % 2 == 0:
                        if n:
                            dve.wait_ge(sems["out_done"] if cross else sems["diff_done"], n // 2)
                        dve.tensor_tensor(first[:, :], ps_o[:, :], inv_sum[:, :], ALU.mult
                                          ).then_inc(sems["output_read"], 1)
                        return
                    dve.tensor_tensor(diff[:, 0, :], ps_o[:, :], inv_sum[:, :], ALU.mult).then_inc(sems["output_read"], 1)

                def combine(key):
                    n = result_at[key]
                    g = n // 2
                    dve.wait_ge(sems["output_read"], n + 1)
                    if cross:
                        if g >= 2:
                            dve.wait_ge(out_stored[g % 2], DMA * (g // 2))
                        dve.tensor_tensor(out[:, g % 2, :], diff[:, 0, :], first[:, :], ALU.add
                                          ).then_inc(sems["out_done"], 1)
                        return
                    dve.scalar_tensor_tensor(diff[:, 1, :], diff[:, 0, :], neg_lam[:, 0:1], first[:, :],
                                             ALU.mult, ALU.add).then_inc(sems["diff_done"], 1)
                    dve.wait_ge(sems["diff_done"], g + 1)
                    if g:
                        dve.wait_ge(sems["rms_done"], g)
                    dve.tensor_tensor(mean_sq[:, 0, :], diff[:, 1, :], diff[:, 1, :], ALU.mult
                                      ).then_inc(sems["squares_done"], 1)

                def finish(g):
                    dve.wait_ge(sems["rms_done"], g + 1)
                    if g >= 2:
                        dve.wait_ge(out_stored[g % 2], DMA * (g // 2))
                    dve.scalar_tensor_tensor(out[:, g % 2, :], diff[:, 1, :], gamma[:, 1:2], mean_sq[:, 1, :],
                                             ALU.mult, ALU.mult).then_inc(sems["out_done"], 1)

                for key in uses[-1]:
                    read(key)
                for st in range(STEPS + 3):
                    finished = [key for key in products.get(st - 1, []) if key in result_at]
                    early_ones = list(uses[st]) if st < STEPS else []
                    for key in finished:
                        normalise(key)
                    for key in early_ones:
                        read(key)
                    for key in finished:
                        if result_at[key] % 2:
                            combine(key)
                    if not cross and st % (2 * TT) == TT + 1 and 2 * TT < st < STEPS:
                        finish(st // (2 * TT) - 1)
                for key in uses[STEPS]:
                    read(key)
                if not cross:
                    finish(NH // 2 - 1)

        loop_over_batch(nc, ctx, names, build, BATCHES)



def middle(nc, t, scratch):
    with ExitStack() as ctx:
        sources = [(("wo", k), t["wo"][k * P:(k + 1) * P, :]) for k in range(EC)]
        sources += [(("xwq", k), t["xwq"][k * P:(k + 1) * P, :]) for k in range(EC)]
        for m in ("xwk", "xwv"):
            sources += [((m, k), t[m][k * P:(k + 1) * P, :]) for k in range(CC)]
        for m, c in (("xwk_dca", 0), ("xwv_dca", E)):
            sources += [((m, k), t["xwkv_dca"][k * P:(k + 1) * P, c:c + E]) for k in range(CC)]
        centre = [p for p, _ in sources if p[0] in ("xwq", "xwk", "xwk_dca")]
        w = split_weights(nc, ctx, "w3", [(E, False, sources)], centre=centre)

        sb = lambda n, shape, dt=F32: ctx.enter_context(nc.sbuf_tensor(f"m_{n}", shape, dt))
        DEPTH = 4
        each = lambda n, shape, dt=F32: [sb(f"{n}{batch}", shape, dt) for batch in range(BATCHES)]
        a_raws = each("a_raw", [P, EC, S])
        y_his, y_los = each("y_hi", [P, EC, S], F32R), each("y_lo", [P, EC, S], F32R)
        c_his, c_los = each("c_hi", [P, CC, S], F32R), each("c_lo", [P, CC, S], F32R)
        x_ins = each("x_in", [P, TT, E])
        centreds = each("centred", [P, DEPTH, S])
        squareses = each("squares", [P, DEPTH, S])
        all_stats, all_moments = each("stats", [P, TT, 6]), each("moments", [P, TT, 2])
        log_vars, rstds = each("log_var", [P, TT]), each("rstd", [P, TT])
        c_raw = sb("c_raw", [P, CC, S])
        normed = sb("normed", [P, 2, S])
        parts = sb("parts", [P, 2, 2, S])
        v = sb("v", [P, 2, E])
        bv = sb("bv", [P, 2, E])
        ident, head_mean, centring = sb("ident", [P, P]), sb("head_mean", [P, P]), sb("centring", [P, P])
        bias_raw, bias = sb("bias_raw", [P, 3, EC]), sb("bias", [P, 3, EC])
        affine = sb("affine", [P, 6])
        masks = sb("masks", [P, 2])
        eps = sb("eps", [P, 2])
        psum = [ctx.enter_context(nc.psum_tensor(f"ps3_{n}", [P, S], F32)) for n in range(8)]

        const_in = ctx.enter_context(nc.semaphore("m_const_in"))
        bias_ready = ctx.enter_context(nc.semaphore("m_bias_ready"))
        with nc.Block() as block:
            @block.sync
            def _(sp):
                for tile, name in ((ident, "ident"), (head_mean, "head_mean"), (centring, "centring"),
                                   (masks, "masks")):
                    sp.dma_start(tile[:, :], t[name]).then_inc(const_in, DMA)
                sp.dma_start(bias_raw[:, :, :], t["head_bias"]).then_inc(const_in, DMA)
                sp.dma_start(affine[:, :], t["head_affine"]).then_inc(const_in, DMA)
                sp.dma_start(bv[:, 0, :], t["xbv"].partition_broadcast(P)).then_inc(const_in, DMA)
                sp.dma_start(bv[:, 1, :], t["xbkv_dca"][E:2 * E].partition_broadcast(P)).then_inc(const_in, DMA)
                sp.wait_ge(const_in, 8 * DMA)

            @block.vector
            def _(dve):
                dve.memset(eps[:, 0:1], LN_EPS)
                dve.memset(eps[:, 1:2], HEAD_EPS)
                dve.wait_ge(bias_ready, 1)
                dve.tensor_copy(bias[:, :, :].rearrange("p n k -> p (n k)"), psum[0][:, 0:3 * EC])

            @block.tensor
            def _(pe):
                pe.wait_ge(const_in, 8 * DMA)
                pe.matmul(psum[0][:, 0:3 * EC], centring[:, :], bias_raw[:, :, :].rearrange("p n k -> p (n k)"),
                          start=True, stop=True).then_inc(bias_ready, 1)

        heads = [("k", j) for j in range(EC)] + [("q", j) for j in range(EC)]
        first_keys = [("wo", n) for n in range(TT)] + [("k", j) for j in range(EC)] + [("v", n) for n in range(TT + 1)]
        second_keys = [("turn", k) for k in range(EC)] + [("kvar", j) for j in range(EC)]
        second_keys += [("q", 0), ("q", 1), ("q", 2), ("qvar", 0), ("q", 3), ("qvar", 1), ("qvar", 2), ("qvar", 3)]
        order = [(batch, *key) for keys in (first_keys, second_keys) for batch in range(BATCHES) for key in keys]
        own = ["a_in", "c_in", "x_in", "a_hi", "a_lo", "c_hi", "c_lo", "z_done", "stats_done", "moments_done",
               "log_done", "rstd_done", "x1_done", "x1_out", "y_hi_done", "y_lo_done", "centred_done",
               "squares_done", "head_log", "scale_done", "scaled_done", "v_done", "vm_done"]
        names = [f"{n}_{batch}" for batch in range(BATCHES) for n in own]
        names += ["normed_done", "hi_done", "lo_done", "parts_out0", "parts_out1", "v_out0", "v_out1"] + Banks.names(8)

        def build(block, b, all_sems):
            bank = Banks(order, psum, all_sems)
            parts_out = [all_sems["parts_out0"], all_sems["parts_out1"]]
            v_out = [all_sems["v_out0"], all_sems["v_out1"]]
            for batch in range(BATCHES):
                loads(block, b, all_sems, batch)
            for phase in (first_phase, second_phase):
                for batch in range(BATCHES):
                    phase(block, b, all_sems, batch, bank, parts_out, v_out)

            @block.sync
            def _(sp):
                for batch in range(BATCHES):
                    sp.wait_ge(all_sems[f"x1_out_{batch}"], DMA)
                for n in range(2):
                    sp.wait_ge(parts_out[n], BATCHES * len(heads) // 2 * DMA)
                    sp.wait_ge(v_out[n], BATCHES * (TT + 1) // 2 * DMA)

        def bank_free(pe, all_sems, bank, batch, key):
            if bank.round((batch, *key)):
                former, m, j = order[bank.at[batch, *key] - 8]
                sems = own_sems(all_sems, own, former)
                if m in ("k", "q"):
                    pe.wait_ge(sems["centred_done"], heads.index((m, j)) + 1)
                elif m == "v":
                    pe.wait_ge(sems["v_done"], min(j + 1, TT - 1))
                    if j >= TT - 1:
                        pe.wait_ge(sems["vm_done"], j - TT + 2)
                elif m == "turn":
                    pe.wait_ge(sems["y_lo_done"], j + 1)
                elif m == "wo":
                    pe.wait_ge(sems["z_done"], j + 1)
                else:
                    pe.wait_ge(sems["head_log"], heads.index((m[0], j)) + 1)

        def loads(block, b, all_sems, batch):
            sems = own_sems(all_sems, own, batch)

            @block.sync
            def _(sp):
                sp.dma_start(a_raws[batch][:, :, :], batch_of(scratch["attn"], b, batch)
                             .rearrange("a k p n -> p (a k) n")).then_inc(sems["a_in"], DMA)
                sp.dma_start(x_ins[batch][:, :, :], batch_of(t["x"], b, batch)
                             .rearrange("a (t p) e -> p (a t) e", p=P)).then_inc(sems["x_in"], DMA)
                if batch:
                    sp.wait_ge(all_sems["c_hi_0"], CC)
                    sp.wait_ge(all_sems["c_lo_0"], CC)
                sp.dma_start(c_raw[:, :, :], batch_of(t["cT"], b, batch)
                             .rearrange("a (k p) n -> p (a k) n", p=P)).then_inc(sems["c_in"], DMA)

            a_raw, y_hi, y_lo = a_raws[batch], y_his[batch], y_los[batch]
            c_hi, c_lo = c_his[batch], c_los[batch]

            @block.scalar
            def _(act):
                nc.scalar.preload_act_table_set(LN_AND_EXP)
                act.wait_ge(sems["a_in"], DMA)
                for k in range(EC):
                    act.activation(y_hi[:, k, :], a_raw[:, k, :], ACT.Copy).then_inc(sems["a_hi"], 1)
                act.wait_ge(sems["c_in"], DMA)
                for k in range(CC):
                    act.activation(c_hi[:, k, :], c_raw[:, k, :], ACT.Copy).then_inc(sems["c_hi"], 1)

            @block.vector
            def _(dve):
                dve.wait_ge(sems["a_in"], DMA)
                for k in range(EC):
                    dve.wait_ge(sems["a_hi"], k + 1)
                    dve.tensor_tensor(y_lo[:, k, :], a_raw[:, k, :], y_hi[:, k, :].bitcast(F32), ALU.subtract
                                      ).then_inc(sems["a_lo"], 1)
                dve.wait_ge(sems["c_in"], DMA)
                for k in range(CC):
                    dve.wait_ge(sems["c_hi"], k + 1)
                    dve.tensor_tensor(c_lo[:, k, :], c_raw[:, k, :], c_hi[:, k, :].bitcast(F32), ALU.subtract
                                      ).then_inc(sems["c_lo"], 1)

        def first_phase(block, b, all_sems, batch, bank, parts_out, v_out):
            sems = own_sems(all_sems, own, batch)
            a_raw, y_hi, y_lo, x_in = a_raws[batch], y_his[batch], y_los[batch], x_ins[batch]
            c_hi, c_lo, centred, squares = c_his[batch], c_los[batch], centreds[batch], squareses[batch]
            stats, moments, log_var, rstd = all_stats[batch], all_moments[batch], log_vars[batch], rstds[batch]
            result = lambda key: bank.tile((batch, *key))

            def full(eng, key):
                eng.wait_ge(bank.full((batch, *key)), bank.round((batch, *key)) + 1)

            @block.sync
            def _(sp):
                for n in range(TT + 1):
                    sp.wait_ge(sems["v_done"], n + 1)
                    slot = (batch * (TT + 1) + n) % 2
                    sp.dma_start(batch_of(scratch["cv"], b, batch)[:, :, n * E:(n + 1) * E]
                                 .rearrange("a p n -> p (a n)"), v[:, slot, :]).then_inc(v_out[slot], DMA)
                sp.wait_ge(sems["x1_done"], TT)
                sp.dma_start(batch_of(scratch["x1"], b, batch).rearrange("a (t p) e -> p (a t) e", p=P),
                             x_in[:, :, :]).then_inc(sems["x1_out"], DMA)

            @block.scalar
            def _(act):
                def centre(n):
                    m, j = heads[n]
                    full(act, (m, j))
                    ps = result((m, j))
                    act.activation(centred[:, n, 0:MAIN], ps[:, 0:MAIN], ACT.Identity, bias=bias[:, 1, j:j + 1])
                    act.activation(centred[:, n, MAIN:S], ps[:, MAIN:S], ACT.Identity,
                                   bias=bias[:, 2, j:j + 1]).then_inc(sems["centred_done"], 1)
                    act.wait_ge(sems["centred_done"], n + 1)
                    act.activation(squares[:, n, :], centred[:, n, :], ACT.Square).then_inc(sems["squares_done"], 1)

                for n in range(EC):
                    centre(n)
                act.wait_ge(sems["moments_done"], TT)
                act.activation(log_var[:, :], moments[:, :, 1], ACT.Ln, bias=eps[:, 0:1]).then_inc(sems["log_done"], 1)
                act.wait_ge(sems["log_done"], 1)
                act.activation(rstd[:, :], log_var[:, :], ACT.Exp, scale=-0.5).then_inc(sems["rstd_done"], 1)

            @block.vector
            def _(dve):
                z = a_raw
                dve.wait_ge(sems["a_lo"], EC)
                dve.wait_ge(sems["x_in"], DMA)
                for n in range(TT):
                    full(dve, ("wo", n))
                    dve.tensor_tensor(z[:, n, :], result(("wo", n))[:, :], x_in[:, n, :], ALU.add
                                      ).then_inc(sems["z_done"], 1)
                    dve.wait_ge(sems["z_done"], n + 1)
                    dve.bn_stats(stats[:, n, :], z[:, n, :]).then_inc(sems["stats_done"], 1)
                    dve.wait_ge(sems["stats_done"], n + 1)
                    dve.bn_aggr(moments[:, n, :], stats[:, n, :]).then_inc(sems["moments_done"], 1)
                dve.wait_ge(sems["moments_done"], TT)
                dve.wait_ge(sems["rstd_done"], 1)
                for n in range(TT):
                    dve.tensor_scalar(x_in[:, n, :], z[:, n, :], moments[:, n, 0:1], rstd[:, n:n + 1],
                                      ALU.subtract, ALU.mult).then_inc(sems["x1_done"], 1)

                for n in range(TT + 1):
                    key = ("v", n)
                    full(dve, key)
                    use = batch * (TT + 1) + n
                    slot = use % 2
                    if use >= 2:
                        dve.wait_ge(v_out[slot], use // 2 * DMA)
                    done = sems["v_done"] if n < TT - 1 else sems["vm_done"]
                    dve.tensor_tensor(v[:, slot, :], result(key)[:, :], bv[:, n // TT, :], ALU.add
                                      ).then_inc(done, 1)
                    if n >= TT - 1:
                        dve.wait_ge(sems["vm_done"], n - TT + 2)
                        dve.tensor_scalar(v[:, slot, :], v[:, slot, :], masks[:, n // TT:n // TT + 1], None,
                                          ALU.mult).then_inc(sems["v_done"], 1)

            @block.tensor
            def _(pe):
                for key in first_keys:
                    m, j = key
                    ps = result(key)
                    bank_free(pe, all_sems, bank, batch, key)
                    if m == "wo":
                        for k in range(EC):
                            pe.wait_ge(sems["a_hi"], k + 1)
                            pe.wait_ge(sems["a_lo"], k + 1)
                            rows = tuple(a[:, k, j * P:(j + 1) * P] for a in (y_hi, y_lo))
                            mm = products_of_parts(pe, ps[:, :], rows, w["wo", k], k == 0, k == EC - 1)
                    elif m == "k":
                        pe.wait_ge(sems["c_hi"], CC)
                        pe.wait_ge(sems["c_lo"], CC)
                        for name, a, z in (("xwk", 0, MAIN), ("xwk_dca", MAIN, S)):
                            for k in range(CC):
                                wk = tuple(x[:, j * P:(j + 1) * P] for x in w[name, k])
                                ck = (c_hi[:, k, a:z], c_lo[:, k, a:z])
                                mm = products_of_parts(pe, ps[:, a:z], wk, ck, k == 0, k == CC - 1)
                    elif m == "v":
                        tile, name = (j, "xwv") if j < TT else (TT - 1, "xwv_dca")
                        for k in range(CC):
                            ck = tuple(a[:, k, tile * P:(tile + 1) * P] for a in (c_hi, c_lo))
                            mm = products_of_parts(pe, ps[:, :], ck, w[name, k], k == 0, k == CC - 1)
                    mm.then_inc(bank.full((batch, *key)), 1)

        def second_phase(block, b, all_sems, batch, bank, parts_out, v_out):
            sems = own_sems(all_sems, own, batch)
            y_hi, y_lo, x_in = y_his[batch], y_los[batch], x_ins[batch]
            centred, squares, scale = centreds[batch], squareses[batch], squareses[batch]
            before = batch * len(heads)
            result = lambda key: bank.tile((batch, *key))

            def full(eng, key):
                eng.wait_ge(bank.full((batch, *key)), bank.round((batch, *key)) + 1)

            @block.sync
            def _(sp):
                for n, (m, j) in enumerate(heads):
                    sp.wait_ge(all_sems["lo_done"], before + n + 1)
                    sp.dma_start(batch_of(scratch["c" + m], b, batch)[:, :, j].rearrange("a k p n -> p (a k) n"),
                                 parts[:, n % 2, :, :]).then_inc(parts_out[n % 2], DMA)

            @block.scalar
            def _(act):
                def centre(n):
                    m, j = heads[n]
                    full(act, (m, j))
                    act.wait_ge(sems["normed_done"], before + n - DEPTH + 1)
                    act.activation(centred[:, n % DEPTH, :], result((m, j))[:, :], ACT.Identity,
                                   bias=bias[:, 0, j:j + 1]).then_inc(sems["centred_done"], 1)
                    act.wait_ge(sems["centred_done"], n + 1)
                    act.wait_ge(sems["scaled_done"], n - DEPTH + 1)
                    act.activation(squares[:, n % DEPTH, :], centred[:, n % DEPTH, :], ACT.Square
                                   ).then_inc(sems["squares_done"], 1)

                def inverse(n):
                    m, j = heads[n]
                    full(act, (m + "var", j))
                    ps = result((m + "var", j))
                    act.activation(scale[:, n % DEPTH, :], ps[:, :], ACT.Ln, bias=eps[:, 1:2]
                                   ).then_inc(sems["head_log"], 1)
                    act.wait_ge(sems["head_log"], n + 1)
                    act.activation(scale[:, n % DEPTH, :], scale[:, n % DEPTH, :], ACT.Exp, scale=-0.5
                                   ).then_inc(sems["scale_done"], 1)

                for k in range(EC):
                    full(act, ("turn", k))
                    act.activation(y_hi[:, k, :], result(("turn", k))[:, :], ACT.Copy).then_inc(sems["y_hi_done"], 1)
                for n in range(len(heads)):
                    inverse(n)
                    if 1 <= n <= EC:
                        centre(EC + n - 1)

            @block.gpsimd
            def _(pool):
                for n in range(len(heads)):
                    pool.wait_ge(sems["normed_done"], before + n + 1)
                    pool.wait_ge(sems["hi_done"], before + n + 1)
                    pool.tensor_tensor(parts[:, n % 2, 1, :].bitcast(F32R), normed[:, n % 2, :],
                                       parts[:, n % 2, 0, :], ALU.subtract).then_inc(sems["lo_done"], 1)

            @block.vector
            def _(dve):
                def affine_norm(n):
                    m, j = heads[n]
                    dve.wait_ge(sems["centred_done"], n + 1)
                    dve.wait_ge(sems["scale_done"], n + 1)
                    dve.tensor_tensor(centred[:, n % DEPTH, :], centred[:, n % DEPTH, :], scale[:, n % DEPTH, :], ALU.mult
                                      ).then_inc(sems["scaled_done"], 1)
                    dve.wait_ge(sems["scaled_done"], n + 1)
                    if before + n >= 2:
                        dve.wait_ge(sems["lo_done"], before + n - 1)
                    if m == "k":
                        dve.tensor_scalar(normed[:, n % 2, 0:MAIN], centred[:, n % DEPTH, 0:MAIN],
                                          affine[:, 2:3], affine[:, 3:4], ALU.mult, ALU.add)
                        dve.tensor_scalar(normed[:, n % 2, MAIN:S], centred[:, n % DEPTH, MAIN:S],
                                          affine[:, 4:5], affine[:, 5:6], ALU.mult, ALU.add
                                          ).then_inc(sems["normed_done"], 1)
                    else:
                        dve.tensor_scalar(normed[:, n % 2, :], centred[:, n % DEPTH, :],
                                          affine[:, 0:1], affine[:, 1:2], ALU.mult, ALU.add
                                          ).then_inc(sems["normed_done"], 1)
                    dve.wait_ge(sems["normed_done"], before + n + 1)
                    if before + n >= 2:
                        dve.wait_ge(parts_out[n % 2], (before + n) // 2 * DMA)
                    dve.tensor_copy(parts[:, n % 2, 0, :].bitcast(F32R), normed[:, n % 2, :]
                                    ).then_inc(sems["hi_done"], 1)

                for k in range(EC):
                    full(dve, ("turn", k))
                    dve.wait_ge(sems["y_hi_done"], k + 1)
                    dve.tensor_tensor(y_lo[:, k, :], result(("turn", k))[:, :], y_hi[:, k, :].bitcast(F32),
                                      ALU.subtract).then_inc(sems["y_lo_done"], 1)
                for n in range(len(heads)):
                    affine_norm(n)

            @block.tensor
            def _(pe):
                for key in second_keys:
                    m, j = key
                    ps = result(key)
                    bank_free(pe, all_sems, bank, batch, key)
                    if m == "turn":
                        pe.wait_ge(sems["x1_done"], TT)
                        for n in range(TT):
                            mm = pe.transpose(ps[:, n * P:(n + 1) * P], x_in[:, n, j * P:(j + 1) * P], ident[:, :])
                    elif m == "q":
                        for k in range(EC):
                            if j == 0:
                                pe.wait_ge(sems["y_lo_done"], k + 1)
                            wk = tuple(x[:, j * P:(j + 1) * P] for x in w["xwq", k])
                            mm = products_of_parts(pe, ps[:, :], wk, (y_hi[:, k, :], y_lo[:, k, :]),
                                                k == 0, k == EC - 1)
                    else:
                        n = heads.index((m[0], j))
                        pe.wait_ge(sems["squares_done"], n + 1)
                        mm = pe.matmul(ps[:, :], head_mean[:, :], squares[:, n % DEPTH, :], start=True, stop=True)
                    mm.then_inc(bank.full((batch, *key)), 1)

        loop_over_batch(nc, ctx, names, build, BATCHES)



def ffn(nc, t, scratch):
    with ExitStack() as ctx:
        ps_y = [ctx.enter_context(nc.psum_tensor(f"ps5_y{n}", [P, S], F32)) for n in range(TT)]
        ps_h = [ctx.enter_context(nc.psum_tensor(f"ps5_h{n}", [P, S], F32)) for n in range(4)]
        w = split_weights(nc, ctx, "w5", [
            (E, False, [(("xwo", k), t["xwo"][k * P:(k + 1) * P, :]) for k in range(EC)]),
            (HID, True, [((m, k), t[m][k * P:(k + 1) * P, :]) for m in ("wg", "wu") for k in range(EC)]),
            (E, True, [(("wd", c), t["wd"][c * P:(c + 1) * P, :]) for c in range(FC)])],
            square_sum=ps_h[0][:, 0:P])
        sb = lambda n, shape, dt=F32: ctx.enter_context(nc.sbuf_tensor(f"f_{n}", shape, dt))
        a_raw = sb("a_raw", [P, EC, S])
        y_hi, y_lo = sb("y_hi", [P, EC, S], F32R), sb("y_lo", [P, EC, S], F32R)
        x_in = sb("x_in", [P, TT, E])
        silu = sb("silu", [P, S])
        hidden = sb("hidden", [P, 2, S])
        h_hi, h_lo = sb("h_hi", [P, 2, S], F32R), sb("h_lo", [P, 2, S], F32R)
        bo, s_down = sb("bo", [P, E]), sb("s_down", [P, E])
        s_up = sb("s_up", [P, 2, FC])
        stats, moments = sb("stats", [P, TT, 6]), sb("moments", [P, TT, 2])
        log_var, rstd, eps = sb("log_var", [P, TT]), sb("rstd", [P, TT]), sb("eps", [P, 1])
        ident = sb("ident", [P, P])
        largest = sb("largest", [P, 2])
        const_in = ctx.enter_context(nc.semaphore("f_const_in"))
        largest_done = ctx.enter_context(nc.semaphore("f_largest_done"))
        with nc.Block() as block:
            @block.sync
            def _(sp):
                sp.dma_start(ident[:, :], t["ident"]).then_inc(const_in, DMA)
                sp.dma_start(bo[:, :], t["xbo"].partition_broadcast(P)).then_inc(const_in, DMA)
                sp.dma_start(s_down[:, :], t["sd"].partition_broadcast(P)).then_inc(const_in, DMA)
                sp.dma_start(s_up[:, :, :], t["s_up"]).then_inc(const_in, DMA)
                sp.wait_ge(const_in, 4 * DMA)

            @block.vector
            def _(dve):
                dve.memset(eps[:, :], LN_EPS)
                dve.tensor_reduce(largest[:, 0:1], ps_h[0][:, 0:P], AX_X, ALU.max).then_inc(largest_done, 1)
                dve.wait_ge(largest_done, 2)
                dve.tensor_reduce(largest[0:1, 1:2], ps_h[1][0:1, 0:P], AX_X, ALU.max)

            @block.tensor
            def _(pe):
                pe.wait_ge(const_in, 4 * DMA)
                pe.wait_ge(largest_done, 1)
                pe.transpose(ps_h[1][0:1, 0:P], largest[:, 0:1], ident[:, :]).then_inc(largest_done, 1)

        order = [("turn", k) for k in range(EC)] + [(m, c) for c in range(FC) for m in ("wg", "wu")]
        names = ["a_in", "x_in", "biased", "a_hi", "a_lo", "wo_full", "z_done", "stats_done", "moments_done",
                 "log_done", "rstd_done", "x2_done", "y_hi_done", "y_lo_done", "silu_done", "hidden_done",
                 "h_hi_done", "h_lo_done", "down_done", "y_full", "scaled_done", "out_done",
                 "out_stored"] + Banks.names(4)

        def build(block, b, sems):
            bank = Banks(order, ps_h, sems)

            def full(eng, key):
                eng.wait_ge(bank.full(key), bank.round(key) + 1)

            @block.sync
            def _(sp):
                sp.dma_start(a_raw[:, :, :], scratch["ctx"][bass.ds(b, 1)].rearrange("a k p n -> p (a k) n")
                             ).then_inc(sems["a_in"], DMA)
                sp.dma_start(x_in[:, :, :], scratch["x1"][bass.ds(b, 1)].rearrange("a (t p) e -> p (a t) e", p=P)
                             ).then_inc(sems["x_in"], DMA)
                sp.wait_ge(sems["out_done"], TT)
                sp.dma_start(t["out"][bass.ds(b, 1)].rearrange("a (t p) e -> p (a t) e", p=P), x_in[:, :, :]
                             ).then_inc(sems["out_stored"], DMA)
                sp.wait_ge(sems["out_stored"], DMA)

            @block.gpsimd
            def _(pool):
                pool.wait_ge(sems["x_in"], DMA)
                for n in range(TT):
                    pool.tensor_tensor(x_in[:, n, :], x_in[:, n, :], bo[:, :], ALU.add).then_inc(sems["biased"], 1)

            @block.scalar
            def _(act):
                act.wait_ge(sems["a_in"], DMA)
                for k in range(EC):
                    act.activation(y_hi[:, k, :], a_raw[:, k, :], ACT.Copy).then_inc(sems["a_hi"], 1)

                def inverse(turn):
                    act.wait_ge(sems["moments_done"], TT * (turn + 1))
                    act.activation(log_var[:, :], moments[:, :, 1], ACT.Ln, bias=eps[:, 0:1]
                                   ).then_inc(sems["log_done"], 1)
                    act.wait_ge(sems["log_done"], turn + 1)
                    act.activation(rstd[:, :], log_var[:, :], ACT.Exp, scale=-0.5).then_inc(sems["rstd_done"], 1)

                inverse(0)
                for k in range(EC):
                    full(act, ("turn", k))
                    act.activation(y_hi[:, k, :], bank.tile(("turn", k))[:, :], ACT.Copy).then_inc(sems["y_hi_done"], 1)
                for c in range(FC):
                    full(act, ("wg", c))
                    if c:
                        act.wait_ge(sems["hidden_done"], c)
                    act.activation(silu[:, :], bank.tile(("wg", c))[:, :], ACT.Silu, scale=s_up[:, 0, c:c + 1]
                                   ).then_inc(sems["silu_done"], 1)
                    act.wait_ge(sems["hidden_done"], c + 1)
                    if c >= 2:
                        act.wait_ge(sems["down_done"], c - 1)
                    act.activation(h_hi[:, c % 2, :], hidden[:, c % 2, :], ACT.Copy).then_inc(sems["h_hi_done"], 1)
                inverse(1)

            @block.vector
            def _(dve):
                dve.wait_ge(sems["a_in"], DMA)
                for k in range(EC):
                    dve.wait_ge(sems["a_hi"], k + 1)
                    dve.tensor_tensor(y_lo[:, k, :], a_raw[:, k, :], y_hi[:, k, :].bitcast(F32), ALU.subtract
                                      ).then_inc(sems["a_lo"], 1)
                z = a_raw
                dve.wait_ge(sems["a_lo"], EC)

                def norm(turn, n):
                    dve.wait_ge(sems["z_done"], TT * turn + n + 1)
                    dve.bn_stats(stats[:, n, :], z[:, n, :]).then_inc(sems["stats_done"], 1)
                    dve.wait_ge(sems["stats_done"], TT * turn + n + 1)
                    dve.bn_aggr(moments[:, n, :], stats[:, n, :]).then_inc(sems["moments_done"], 1)

                def scale(turn, done):
                    dve.wait_ge(sems["moments_done"], TT * (turn + 1))
                    dve.wait_ge(sems["rstd_done"], turn + 1)
                    for n in range(TT):
                        dve.tensor_scalar(x_in[:, n, :], z[:, n, :], moments[:, n, 0:1], rstd[:, n:n + 1],
                                          ALU.subtract, ALU.mult).then_inc(done, 1)

                for n in range(TT):
                    dve.wait_ge(sems["wo_full"], n + 1)
                    dve.wait_ge(sems["biased"], n + 1)
                    dve.tensor_tensor(z[:, n, :], ps_y[n][:, :], x_in[:, n, :], ALU.add).then_inc(sems["z_done"], 1)
                    norm(0, n)
                scale(0, sems["x2_done"])
                for k in range(EC):
                    full(dve, ("turn", k))
                    dve.wait_ge(sems["y_hi_done"], k + 1)
                    dve.tensor_tensor(y_lo[:, k, :], bank.tile(("turn", k))[:, :], y_hi[:, k, :].bitcast(F32),
                                      ALU.subtract).then_inc(sems["y_lo_done"], 1)
                for c in range(FC):
                    full(dve, ("wu", c))
                    dve.wait_ge(sems["silu_done"], c + 1)
                    if c >= 2:
                        dve.wait_ge(sems["h_hi_done"], c - 1)
                        dve.wait_ge(sems["h_lo_done"], c - 1)
                    dve.scalar_tensor_tensor(hidden[:, c % 2, :], bank.tile(("wu", c))[:, :], s_up[:, 1, c:c + 1],
                                             silu[:, :], ALU.mult, ALU.mult).then_inc(sems["hidden_done"], 1)
                    dve.wait_ge(sems["hidden_done"], c + 1)
                    dve.wait_ge(sems["h_hi_done"], c + 1)
                    dve.tensor_tensor(h_lo[:, c % 2, :], hidden[:, c % 2, :], h_hi[:, c % 2, :].bitcast(F32),
                                      ALU.subtract).then_inc(sems["h_lo_done"], 1)
                dve.wait_ge(sems["x2_done"], TT)
                for n in range(TT):
                    dve.wait_ge(sems["y_full"], n + 1)
                    dve.tensor_tensor(z[:, n, :], ps_y[n][:, :], s_down[:, :], ALU.mult).then_inc(sems["scaled_done"], 1)
                    dve.wait_ge(sems["scaled_done"], n + 1)
                    dve.tensor_tensor(z[:, n, :], z[:, n, :], x_in[:, n, :], ALU.add).then_inc(sems["z_done"], 1)
                    norm(1, n)
                scale(1, sems["out_done"])

            @block.tensor
            def _(pe):
                for n in range(TT):
                    for k in range(EC):
                        pe.wait_ge(sems["a_hi"], k + 1)
                        pe.wait_ge(sems["a_lo"], k + 1)
                        rows = tuple(a[:, k, n * P:(n + 1) * P] for a in (y_hi, y_lo))
                        mm = products_of_parts(pe, ps_y[n][:, :], rows, w["xwo", k], k == 0, k == EC - 1)
                    mm.then_inc(sems["wo_full"], 1)
                pe.wait_ge(sems["x2_done"], TT)
                for k in range(EC):
                    ps = bank.tile(("turn", k))
                    for n in range(TT):
                        mm = pe.transpose(ps[:, n * P:(n + 1) * P], x_in[:, n, k * P:(k + 1) * P], ident[:, :])
                    mm.then_inc(bank.full(("turn", k)), 1)

                def down(c, terms):
                    pe.wait_ge(sems["h_hi_done"], c + 1)
                    pe.wait_ge(sems["h_lo_done"], c + 1)
                    if c == 0:
                        pe.wait_ge(sems["z_done"], TT)
                    for n in range(TT):
                        rows = (h_hi[:, c % 2, n * P:(n + 1) * P], h_lo[:, c % 2, n * P:(n + 1) * P])
                        mm = products_of_parts(pe, ps_y[n][:, :], rows, w["wd", c], c == 0, c == FC - 1, terms)
                        if c == FC - 1:
                            mm.then_inc(sems["y_full"], 1)
                    if c < FC - 1:
                        mm.then_inc(sems["down_done"], 1)

                def network(up_terms, down_terms):
                    for c in range(FC):
                        for i, m in enumerate(("wg", "wu")):
                            key = (m, c)
                            use = bank.at[key]
                            if use < 8:
                                if use >= 4:
                                    pe.wait_ge(sems["y_lo_done"], use - 3)
                            if c >= 2:
                                pe.wait_ge(sems["silu_done"] if i == 0 else sems["hidden_done"], c - 1)
                            for k in range(EC):
                                pe.wait_ge(sems["y_hi_done"], k + 1)
                                pe.wait_ge(sems["y_lo_done"], k + 1)
                                wk = tuple(a[:, c * P:(c + 1) * P] for a in w[m, k])
                                mm = products_of_parts(pe, bank.tile(key)[:, :], wk, (y_hi[:, k, :], y_lo[:, k, :]),
                                                       k == 0, k == EC - 1, up_terms)
                            mm.then_inc(bank.full(key), 1)
                        if c:
                            down(c - 1, down_terms)
                    down(FC - 1, down_terms)

                lo_parts = pe.value_load(largest[0:1, 1:2].bitcast(I32))
                with pe.If(lo_parts != 0):
                    network(THREE, THREE)
                with pe.Else():
                    network(STATIONARY_WHOLE, MOVING_WHOLE)

        loop_over_batch(nc, ctx, names, build)


def build(nc, t):
    scratch = {}
    for name, shape in (("q", (B, 2, 2, 2 * P, S)), ("k", (B, 2, 2, 2 * P, S)), ("v", (B, P, TT * E)),
                        ("attn", (B, EC, P, S)), ("x1", (B, S, E)), ("cq", (B, 2, EC, P, S)),
                        ("ck", (B, 2, EC, P, S)), ("cv", (B, P, (TT + 1) * E)), ("ctx", (B, EC, P, S))):
        scratch[name] = nc.dram_tensor(f"scratch_{name}", shape, F32).ap()
    self_projections(nc, t, scratch)
    attention(nc, t, scratch, "self")
    middle(nc, t, scratch)
    attention(nc, t, scratch, "cross")
    ffn(nc, t, scratch)



def rope_order(np):
    f = np.arange(E).reshape(2, 2, G, 2, PAIRS, 2)
    return f.transpose(0, 5, 1, 3, 2, 4).reshape(E)


def kernel(**inputs):
    import numpy as np
    import concourse.bacc as bacc
    from concourse.bass_utils import run_bass_kernel_spmd

    a = {k: np.asarray(v) for k, v in inputs.items()}
    order = rope_order(np)
    kv = np.concatenate([a["L0_xattn_Wk"], a["L0_xattn_Wv"]], -1).reshape(CD, H, 2, HW)
    bkv = np.concatenate([a["L0_xattn_bk"], a["L0_xattn_bv"]]).reshape(H, 2, HW)
    head_biases = (a["L0_xattn_bq"], bkv[:, 0].reshape(E), a["L0_xattn_bkv_dca"][:E])
    arrays = {
        "x": a["x"], "xT": a["x"].transpose(0, 2, 1), "cT": a["ctx_1024"].transpose(0, 2, 1),
        "wq": a["L0_attn_Wq"].T[:, order], "wk": a["L0_attn_Wk"].T[:, order],
        "wv": a["L0_attn_Wv"].T, "wo": a["L0_attn_Wo"].T,
        "xwq": a["L0_xattn_Wq"], "xwk": kv[:, :, 0].reshape(CD, E), "xwv": kv[:, :, 1].reshape(CD, E),
        "xwkv_dca": a["L0_xattn_Wkv_dca"], "xwo": a["L0_xattn_Wo"],
        "wg": a["L0_ffn_wq_gate"].T, "wu": a["L0_ffn_wq_up"].T, "wd": a["L0_ffn_wq_down"].T,
        "sd": a["L0_ffn_s_down"], "xbv": bkv[:, 1].reshape(E), "xbo": a["L0_xattn_bo"],
        "xbkv_dca": a["L0_xattn_bkv_dca"],
        "s_up": np.stack([a["L0_ffn_" + n].reshape(FC, P).T for n in ("s_gate", "s_up")], 1),
        "gamma": np.tile(a["L0_attn_gamma"], G)[:, None],
        "head_bias": np.stack([v.reshape(EC, P).T for v in head_biases], 1),
        "head_affine": np.stack([np.tile(a["L0_xattn_" + n], G) for n in
                                 ("qn_w", "qn_b", "kn_w", "kn_b", "kn_dca_w", "kn_dca_b")], 1),
    }
    for n in ("lambda_q1", "lambda_k1", "lambda_q2", "lambda_k2"):
        arrays[n] = a["L0_attn_" + n]

    f = np.float32
    angle = (f(1.0) / np.power(f(2500.0), np.linspace(0.0, 1.0, PAIRS, dtype=f))).astype(f)
    phase = (np.arange(S, dtype=f)[None, :] * angle[:, None]).astype(f).astype(np.float64)
    arrays["trig"] = np.tile(np.stack([np.cos(phase), np.sin(phase)], 1), (P // PAIRS, 1, 1)).astype(f)
    arrays["ident"] = np.eye(P, dtype=f)
    arrays["head_mean"] = np.kron(np.eye(G), np.full((HW, HW), 1.0 / HW)).astype(f)
    arrays["centring"] = arrays["ident"] - arrays["head_mean"]
    main = (np.arange(S) < MAIN).astype(f)
    arrays["key_rows"] = np.stack([main, main, 1 - main, 1 - main])
    arrays["masks"] = np.stack([main[-P:], 1 - main[-P:]], 1)

    nc = bacc.Bacc("TRN2", target_bir_lowering=False, num_devices=1)
    arrays = {n: np.ascontiguousarray(v) for n, v in arrays.items()}
    t = {n: nc.dram_tensor(f"in_{n}", v.shape, mybir.dt.from_np(v.dtype), kind="ExternalInput").ap()
         for n, v in arrays.items()}
    t["out"] = nc.dram_tensor("result", (B, S, E), F32, kind="ExternalOutput").ap()
    build(nc, t)
    r = run_bass_kernel_spmd(nc, [{f"in_{n}": v for n, v in arrays.items()}], core_ids=[0])
    return r.results[0]["result"]
```
